# Optimizing a Trainium2 kernel written in Bass

```python
import numpy as np
import jax
import jax.numpy as jnp

def _softmax(x, axis=-1):
    return jax.nn.softmax(x, axis=axis)

def _gelu(x):
    return jax.nn.gelu(x, approximate=True)

def _silu(x):
    return jax.nn.silu(x)

def _sigmoid(x):
    return jax.nn.sigmoid(x)

def _layernorm(x, axis=-1, eps=1e-05):
    m = jnp.mean(x, axis=axis, keepdims=True)
    v = jnp.var(x, axis=axis, keepdims=True)
    return (x - m) / jnp.sqrt(v + eps)

def _scatter_add(tgt, idx, src, axis=0):
    return tgt.at[idx].add(src)

def _segment_sum(src, seg, n):
    return jax.ops.segment_sum(src, seg, n)
kernel_name = 'mk_seq_postln_d1_jaxref_r8_bf8921'

def setup_inputs(seed: int=0):
    np.random.seed(seed)
    _w = jnp.asarray

    def _L0_attn_setup():
        import jax, jax.numpy as jnp
        import numpy as np
        DIM = 128
        HEADS = 16
        DIM_HEAD = 64
        key = jax.random.key(seed)
        ks = jax.random.split(key, 6)
        inner = HEADS * DIM_HEAD
        s = lambda fan_in: 1.0 / np.sqrt(fan_in)
        return {'x': jax.random.normal(ks[0], (4, 512, DIM), dtype=jnp.float32), 'W_qkv': jax.random.normal(ks[1], (DIM, inner * 3), dtype=jnp.float32) * s(DIM), 'W_f': jax.random.normal(ks[2], (DIM_HEAD, DIM_HEAD), dtype=jnp.float32) * s(DIM_HEAD), 'b_f': jax.random.normal(ks[3], (DIM_HEAD,), dtype=jnp.float32) * 0.01, 'W_out': jax.random.normal(ks[4], (inner, DIM), dtype=jnp.float32) * s(inner), 'b_out': jax.random.normal(ks[5], (DIM,), dtype=jnp.float32) * 0.01}
    _L0_attn_in = _L0_attn_setup()

    def _L0_ffn_setup():
        import jax, jax.numpy as jnp
        import numpy as np
        NUM_EXPERTS = 8
        TOP_K = 2
        key = jax.random.key(seed)
        ks = jax.random.split(key, 6)
        B, S, D, F = (2, 256, 128, 512)
        E = NUM_EXPERTS
        sd = 1.0 / np.sqrt(D)
        sf = 1.0 / np.sqrt(F)
        return {'x': jax.random.normal(ks[0], (B, S, D), dtype=jnp.float32), 'gate_w': jax.random.normal(ks[1], (E, D), dtype=jnp.float32) * sd, 'w1': jax.random.uniform(ks[2], (F, E, D), dtype=jnp.float32, minval=-sd, maxval=sd), 'b1': jax.random.uniform(ks[3], (E, F), dtype=jnp.float32, minval=-sd, maxval=sd), 'w2': jax.random.uniform(ks[4], (D, E, F), dtype=jnp.float32, minval=-sf, maxval=sf), 'b2': jax.random.uniform(ks[5], (E, D), dtype=jnp.float32, minval=-sf, maxval=sf)}
    _L0_ffn_in = _L0_ffn_setup()
    _d = {'L0_attn_x': _L0_attn_in['x'], 'L0_attn_W_qkv': _L0_attn_in['W_qkv'], 'L0_attn_W_f': _L0_attn_in['W_f'], 'L0_attn_b_f': _L0_attn_in['b_f'], 'L0_attn_W_out': _L0_attn_in['W_out'], 'L0_attn_b_out': _L0_attn_in['b_out'], 'L0_ffn_gate_w': _L0_ffn_in['gate_w'], 'L0_ffn_w1': _L0_ffn_in['w1'], 'L0_ffn_b1': _L0_ffn_in['b1'], 'L0_ffn_w2': _L0_ffn_in['w2'], 'L0_ffn_b2': _L0_ffn_in['b2']}
    _x0 = _d['L0_attn_x']
    _d['L0_attn_x'] = jax.random.normal(jax.random.fold_in(jax.random.key(seed), 1), (8, 512, 128), dtype=_x0.dtype)
    del _x0
    return _d

def reference(L0_attn_x, L0_attn_W_qkv, L0_attn_W_f, L0_attn_b_f, L0_attn_W_out, L0_attn_b_out, L0_ffn_gate_w, L0_ffn_w1, L0_ffn_b1, L0_ffn_w2, L0_ffn_b2):

    def _L0_attn_ref(x, W_qkv, W_f, b_f, W_out, b_out):
        import jax, jax.numpy as jnp
        import numpy as np
        DIM = 128
        HEADS = 16
        DIM_HEAD = 64
        B, N, C = x.shape
        H, D = (HEADS, DIM_HEAD)
        qkv = x @ W_qkv
        q, k, v = jnp.split(qkv, 3, axis=-1)
        reshape = lambda t: t.reshape(B, N, H, D).transpose(0, 2, 1, 3)
        q, k, v = (reshape(q), reshape(k), reshape(v))
        fmap = lambda t: jax.nn.relu(t @ W_f + b_f)
        q = fmap(q)
        k = fmap(k)
        kv = jnp.einsum('bhnd,bhne->bhde', k, v)
        out = jnp.einsum('bhnd,bhde->bhne', q, kv)
        k_sum = k.sum(axis=2)
        normalizer = jnp.einsum('bhnd,bhd->bhn', q, k_sum)
        out = out / (normalizer[..., None] + 1e-06)
        out = out.transpose(0, 2, 1, 3).reshape(B, N, H * D)
        return out @ W_out + b_out

    def _L0_ffn_ref(x, gate_w, w1, b1, w2, b2):
        import jax, jax.numpy as jnp
        import numpy as np
        NUM_EXPERTS = 8
        TOP_K = 2
        logits = jnp.einsum('bsd,ed->bse', x, gate_w)
        probs = jax.nn.softmax(logits, axis=-1)
        topk_probs, topk_idx = jax.lax.top_k(probs, TOP_K)
        oh = jax.nn.one_hot(topk_idx, NUM_EXPERTS, dtype=x.dtype)
        h = jnp.einsum('bsd,fed,bske->bskf', x, w1, oh)
        h = h + jnp.take(b1, topk_idx, axis=0)
        h = jax.nn.gelu(h)
        y = jnp.einsum('bskf,def,bske->bskd', h, w2, oh)
        y = y + jnp.take(b2, topk_idx, axis=0)
        out = jnp.sum(y * topk_probs[..., None], axis=-2)
        return out
    x = L0_attn_x
    x = _layernorm(x + _L0_attn_ref(x, L0_attn_W_qkv, L0_attn_W_f, L0_attn_b_f, L0_attn_W_out, L0_attn_b_out), axis=-1)
    x = _layernorm(x + _L0_ffn_ref(x, L0_ffn_gate_w, L0_ffn_w1, L0_ffn_b1, L0_ffn_w2, L0_ffn_b2), axis=-1)
    return x

_drawn_inputs = setup_inputs


def setup_inputs(seed=0):
    import zlib

    import numpy as np

    out = dict(_drawn_inputs(seed))
    spreads = {}
    factors = {'L0_attn_b_f': 8.0, 'L0_attn_b_out': 4.464, 'L0_ffn_b1': 7.025, 'L0_ffn_b2': 4.959}
    for name, (base, spread) in spreads.items():
        noise = np.random.default_rng([zlib.crc32(name.encode()), seed]).standard_normal(out[name].shape)
        drawn = base * np.exp(spread * noise) if base else spread * noise
        out[name] = jnp.asarray(drawn.astype(out[name].dtype))
    for name, factor in factors.items():
        out[name] = (out[name] * factor).astype(out[name].dtype)
    return out
```

```python
from contextlib import ExitStack

import numpy as np

import concourse.bass as bass
from concourse import mybir

ALU = mybir.AluOpType
ACT = mybir.ActivationFunctionType
AX_X = mybir.AxisListType.X
F32 = mybir.dt.float32
F32R = mybir.dt.float32r
BF16 = mybir.dt.bfloat16
I32 = mybir.dt.int32
U32 = mybir.dt.uint32
ds = bass.ds

P = 128
D = 128
B, S = 8, 512
N = B * S
TILES = S // P
H, DH = 16, 64
HD = H * DH
CH = HD // P
E, F = 8, 512
FC = F // P
TOPK = 2
BLK = 256
NBLK = (N * TOPK + E * (BLK - 1)) // BLK
REGION = N + BLK
ROW = D + 4
FILL = 4
XS_ROWS = E * REGION + 1024
NOWHERE = E * REGION
LN_EPS = 1e-5
NORM_EPS = 1e-6
RSQRT_SEED = float(0x5F3759DF)
SLOTS = 4
W1_ROW = F + FC

_C = {}
_at = 0
for _name, _n in (("ident", P), ("tri", P), ("ones", P), ("mask", CH * H), ("iota", E), ("dest", TILES * TOPK),
                  ("first", E), ("sel", CH * P), ("block", NBLK), ("step", E * 16), ("upto", E * E)):
    _C[_name] = (_at, _at + _n)
    _at += _n
C_COLS = _at


def shape_constants():
    c = np.zeros((P, C_COLS), np.float32)

    def put(name, value):
        lo, hi = _C[name]
        value = np.asarray(value, np.float32).reshape(-1, hi - lo)
        c[:len(value) if len(value) > 1 else P, lo:hi] = value
    p = np.arange(P)
    put("ident", np.eye(P))
    put("tri", p[:, None] < p[None, :])
    put("ones", np.ones((P, P)))
    put("mask", (p[:, None, None] // DH + 2 * np.arange(CH)[None, :, None] == np.arange(H)[None, None, :]))
    put("iota", np.arange(E)[None])
    put("dest", p[:, None, None] + P * np.arange(TILES)[None, :, None] + N * np.arange(TOPK)[None, None, :])
    put("first", (REGION * np.arange(E))[None])
    r = np.arange(3 * H)
    put("sel", (r[:, None, None] % H == 2 * np.arange(CH)[None, :, None] + p[None, None, :] // DH))
    put("block", np.arange(NBLK)[None])
    put("step", np.broadcast_to(BLK * np.arange(16)[None, :], (E, 16)).reshape(1, -1))
    put("upto", (np.arange(E)[None, :] <= np.arange(E)[:, None]).reshape(1, -1))
    return c



def program(nc, x, xT, wqkvT, wf, bf, wout, bout, gwT, w1, w2, b2, consts, out):
    ctx = ExitStack()
    with ctx:
        def sb(name, shape, dt=F32):
            return ctx.enter_context(nc.sbuf_tensor(name, shape, dt))

        def pb(name, shape, dt=F32):
            return ctx.enter_context(nc.psum_tensor(name, shape, dt))

        def sem(name):
            return ctx.enter_context(nc.semaphore(name))

        xs = nc.dram_tensor("expert_rows", [XS_ROWS, ROW], F32, kind="Internal").ap()
        ys = nc.dram_tensor("expert_results", [TOPK * N, D], F32, kind="Internal").ap()
        b2p = nc.dram_tensor("b2_parts", [3, E * D], BF16, kind="Internal").ap()

        cst = sb("cst", [P, C_COLS])

        def con(name, rows=P):
            lo, hi = _C[name]
            return cst[0:rows, lo:hi]
        x_raw = sb("x_raw", [P, B * TILES, D])
        xT_raw = sb("xT_raw", [P, N])
        x1 = sb("x1", [P, B * TILES, D])
        wq_hi, wq_lo = sb("wq_hi", [P, HD], F32R), sb("wq_lo", [P, HD], F32R)
        wk_hi, wk_lo = sb("wk_hi", [P, HD], F32R), sb("wk_lo", [P, HD], F32R)
        vo_hi, vo_lo = sb("vo_hi", [P, H * D], F32R), sb("vo_lo", [P, H * D], F32R)
        xT_hi, xT_lo = sb("xT_hi", [P, S], F32R), sb("xT_lo", [P, S], F32R)
        x_hi, x_lo = sb("x_hi", [P, TILES, D], F32R), sb("x_lo", [P, TILES, D], F32R)
        k_hi, k_lo = sb("k_hi", [P, TILES, HD], F32R), sb("k_lo", [P, TILES, HD], F32R)
        q_act = sb("q_act", [P, CH, S])
        g_hi, g_lo = sb("g_hi", [P, HD], F32R), sb("g_lo", [P, HD], F32R)
        m_hi, m_lo = sb("m_hi", [P, CH, D], F32R), sb("m_lo", [P, CH, D], F32R)
        qn = sb("qn", [P, 2, S])
        qn_hi, qn_lo = sb("qn_hi", [P, 2, S], F32R), sb("qn_lo", [P, 2, S], F32R)
        zT = sb("zT", [P, S])
        rows = sb("rows", [P, TILES, TOPK, ROW])
        zeros = sb("zeros", [P, FILL, ROW])
        wfd = sb("wfd", [P, P])
        bf_col = sb("bf_col", [P, 1])
        bout_col = sb("bout_col", [P, 1])
        gw = sb("gw", [P, E])
        gwc = sb("gwc", [P, E])
        ones_r = sb("ones_r", [P, 2], F32R)
        ones_b = sb("ones_b", [P, P], BF16)
        tri_b = sb("tri_b", [P, P], BF16)
        ident_b = sb("ident_b", [P, P], BF16)
        sel_b = sb("sel_b", [3 * H, CH, P], BF16)
        parts = sb("parts", [65, S + E * D], BF16)
        ksd = sb("ksd", [P, CH, H])
        rn = sb("rn", [P, 3, TILES, H])
        rparts = sb("rparts", [P, TILES, 3, H], BF16)
        rT = sb("rT", [3 * H, S], BF16)
        stats = sb("stats", [P, TILES, 6])
        mv = sb("mv", [P, TILES, 2])
        ln = sb("ln", [P, 4, TILES])
        logit = sb("logit", [P, TILES, E])
        top = sb("top", [P, TILES, 8])
        topi = sb("topi", [P, TILES, 8], U32)
        topd = sb("topd", [P, TILES, 8])
        tope = sb("tope", [P, TILES, 8])
        den = sb("den", [P, 2, TILES])
        topf = sb("topf", [P, TILES, TOPK])
        hot = sb("hot", [P, TILES, TOPK, E])
        hot_sum = sb("hot_sum", [P, TILES + 1, E], BF16)
        rank = sb("rank", [P, TILES, E])
        picked = sb("picked", [P, TILES, TOPK, E])
        posf = sb("posf", [P, TILES, TOPK])
        pos = sb("pos", [P, TILES, TOPK], I32)
        base = sb("base", [P, E])
        dest = sb("dest", [P, TILES, TOPK])
        cnt = sb("cnt", [1, 3, E])
        full = sb("full", [1, E, 16])
        upto_n = sb("upto_n", [1, E, E])
        past = sb("past", [1, 2, NBLK, E])
        tab = sb("tab", [1, 5, NBLK])
        tabi = sb("tabi", [1, 2, NBLK], I32)
        xrow = [sb(f"xrow{u}", [P, 2, ROW]) for u in range(SLOTS)]
        w1_raw = [sb(f"w1_raw{u}", [P, W1_ROW]) for u in range(SLOTS)]
        b2_row = [sb(f"b2_row{u}", [3, D], BF16) for u in range(SLOTS)]
        wqkvT_sb = q_act[:, :, :].rearrange("p c s -> p (c s)")[:, 0:3 * HD].rearrange("p (c d) -> p c d", d=D)
        woutd = x1[:, 0:2 * CH, :].rearrange("p (c a) d -> p c a d", a=2)
        bias_raw = x1[0:65, 2 * CH:2 * CH + (S + E * D) // D, :].rearrange("p c d -> p (c d)")
        bias_part = qn[0:65, :, :].rearrange("p c s -> p (c s)").bitcast(BF16)[:, 0:S + E * D]
        hT = [q_act[:, FC * v:FC * v + FC, 0:BLK] for v in range(2)]
        w2_raw = [x_raw[:, FC * u:FC * u + FC, :] for u in range(SLOTS)]
        yrow = [x_raw[:, FC * SLOTS + 2 * u:FC * SLOTS + 2 * u + 2, :] for u in range(SLOTS)]
        ya = x_raw
        yb = xT_raw[:, :].rearrange("p (t d) -> p t d", d=D)

        psA = pb("psA", [P, 2, 1024])
        psG = pb("psG", [P, 2, 512])
        psO = pb("psO", [P, 512])
        psS = pb("psS", [P, 512])
        psS_k = psS[:, 0:2 * CH].rearrange("p (c n) -> p c n", n=2)
        psS_n = psS[:, 64:64 + TILES * H].rearrange("p (t h) -> p t h", h=H)
        psS_l = psS[:, 128:128 + TILES * E].rearrange("p (t e) -> p t e", e=E)
        psS_r = psS[0:3 * H, 256:512].bitcast(BF16)
        psO_z = psO[:, :].rearrange("p (t d) -> p t d", d=D)
        psO_c = psO[:, 0:(TILES + 1) * E].rearrange("p (t e) -> p t e", e=E)
        psX = [psG[:, v, 0:BLK] for v in range(2)]
        psH = [psA[:, v, :].rearrange("p (c s) -> p c s", c=FC) for v in range(2)]
        psY = [ps[:, 0:2 * D].rearrange("p (t d) -> p t d", d=D) for ps in (psO, psS)]

        in_c, in_fold, in_x0, in_x, in_small, in_bias = (sem(n) for n in ("in_c", "in_fold", "in_x0", "in_x", "in_small", "in_bias"))
        cleared, bias_cleared, zero_ready, filled, b2_stored = (sem(n) for n in ("cleared", "bias_cleared", "zero_ready", "filled", "b2_stored"))
        cast, bias_step, fold_pe, fold_hi, fold_lo, mean_pe, gwc_ready = (
            sem(n) for n in ("cast", "bias_step", "fold_pe", "fold_hi", "fold_lo", "mean_pe", "gwc_ready"))
        xT_h, xT_l, x_h, x_l = (sem(n) for n in ("xT_h", "xT_l", "x_h", "x_l"))
        k_pe, k_h, k_l, q_pe, q_done, g_pe, g_h, g_l, m_pe, m_h, m_l = (
            sem(n) for n in ("k_pe", "k_h", "k_l", "q_pe", "q_done", "g_pe", "g_h", "g_l", "m_pe", "m_h", "m_l"))
        ks_pe, ks_done, n_pe, n_step, rT_pe, rT_done, bc_pe, qn_done, qn_h, qn_l, o_pe, zT_done = (
            sem(n) for n in ("ks_pe", "ks_done", "n_pe", "n_step", "rT_pe", "rT_done", "bc_pe", "qn_done", "qn_h", "qn_l", "o_pe", "zT_done"))
        z_pe, l_pe, c_pe, st_step, ln_step, x1_done, route, exp_done, scattered, table = (
            sem(n) for n in ("z_pe", "l_pe", "c_pe", "st_step", "ln_step", "x1_done", "route", "exp_done", "scattered", "table"))
        e_x, e_w, e_v, e_out = ([sem(f"{n}{u}") for u in range(SLOTS)] for n in ("e_x", "e_w", "e_v", "e_out"))
        e_T, e_Th, e_Tl, e_wh, e_wl, e_up, e_gelu, e_down, e_y0, e_y = (
            sem(n) for n in ("e_T", "e_Th", "e_Tl", "e_wh", "e_wl", "e_up", "e_gelu", "e_down", "e_y0", "e_y"))
        m_l0, tab_step = sem("m_l0"), sem("tab_step")
        f_in, f_sum, f_st, f_out = ([sem(f"{n}{u}") for u in range(2)] for n in ("f_in", "f_sum", "f_st", "f_out"))
        f_z, f_stats, f_ln, f_norm = (sem(n) for n in ("f_z", "f_stats", "f_ln", "f_norm"))

        N_STEPS, LN_STEPS, ST_STEPS, ROUTE_STEPS = 6, 15, 2 * TILES, 24
        TOP_AT, HOT_AT = 10, 13

        class Steps:

            def __init__(self, eng, which, done):
                self.eng, self.which, self.n = eng, which, done

            def __call__(self, ins):
                ins.then_inc(self.which, 1)
                self.n = self.n + 1

            def wait(self):
                self.eng.wait_ge(self.which, self.n)

        def wait_alone(eng, which, value):
            eng.wait_ge(which, value)
            eng.nop(nofuse=True)

        def batches(eng, body):
            body(0, False, True)
            body(1, True, True)
            with eng.Fori(2, B) as b:
                body(b, True, True)
            body(B, True, False)

        def blocks(eng, body):
            for u in range(SLOTS):
                body(u, u, 0)
            with eng.Fori(1, NBLK // SLOTS) as i:
                for u in range(SLOTS):
                    body(SLOTS * i + u, u, i)
            for u in range(NBLK % SLOTS):
                body(NBLK // SLOTS * SLOTS + u, u, NBLK // SLOTS)

        def earlier(n, u, i, back):
            return n - back, (u - back) % SLOTS, i - (u < back)

        last_blocks = [(n, n % SLOTS, n // SLOTS) for n in (NBLK - 2, NBLK - 1)]

        def later(n, least):
            return not isinstance(n, int) or n >= least

        def pairs(eng, body):
            for u in range(2):
                body(u, u, 0)
            with eng.Fori(1, B // 2) as i:
                for u in range(2):
                    body(2 * i + u, u, i)

        block = ctx.enter_context(nc.Block())

        @block.sync
        def _(sp):
            sp.wait_ge(cleared, 2)
            sp.dma_start(wqkvT_sb, wqkvT.rearrange("(c p) d -> p c d", p=P)).then_inc(in_fold, 16)
            for r in (0, DH):
                sp.dma_start(wfd[r:r + DH, r:r + DH], wf).then_inc(in_fold, 16)
            wout_v = wout.rearrange("(c a p) n -> a p c n", a=2, p=DH)
            for a in range(2):
                sp.dma_start(woutd[DH * a:DH * a + DH, :, a, :], wout_v[a]).then_inc(in_fold, 16)
            x_v = x.rearrange("(t p) d -> p t d", p=P)
            sp.dma_start(xT_raw[:, 0:S], xT[:, 0:S]).then_inc(in_x0, 16)
            sp.dma_start(x_raw[:, 0:TILES, :], x_v[:, 0:TILES, :]).then_inc(in_x0, 16)
            sp.dma_start(xT_raw[:, S:], xT[:, S:]).then_inc(in_x, 16)
            sp.dma_start(x_raw[:, TILES:, :], x_v[:, TILES:, :]).then_inc(in_x, 16)
            sp.wait_ge(zero_ready, 2)
            sp.dma_start(xs.rearrange("(p r f) c -> p r (f c)", p=P, f=FILL),
                         zeros[:, :, :].rearrange("p f c -> p (f c)")[:, None, :]
                         .broadcast_to([P, XS_ROWS // P // FILL, FILL * ROW])).then_inc(filled, 16)
            sp.wait_ge(bias_step, 9)
            for i, r in enumerate((0, 32, 64)):
                sp.dma_start(b2p[i:i + 1, :], parts[r:r + 1, S:]).then_inc(b2_stored, 16)

            sp.wait_ge(b2_stored, 48)
            sp.wait_ge(scattered, 16 * TILES * TOPK * B)
            sp.wait_ge(table, 2)

            def load(n, u, i):
                expert = sp.value_load(tabi[0:1, 0, ds(n, 1)], min_val=0, max_val=E - 1)
                first = sp.value_load(tabi[0:1, 1, ds(n, 1)], min_val=0, max_val=NOWHERE)
                if later(n, SLOTS):
                    wait_alone(sp, e_down, n - SLOTS + 1)
                    wait_alone(sp, e_y, n - SLOTS + 1)
                    wait_alone(sp, e_out[u], 32 * i)
                sp.dma_start(xrow[u][:, :, :], xs[ds(first, BLK), :].rearrange("(c p) d -> p c d", p=P)).then_inc(e_x[u], 16)
                sp.dma_start(w1_raw[u][:, :], w1[ds(expert, 1), :, :].rearrange("a p n -> (a p) n")).then_inc(e_w[u], 16)
                sp.dma_start(w2_raw[u][:, :, :], w2[ds(expert, 1), :, :].rearrange("a p (c n) -> (a p) c n", c=FC)).then_inc(e_v[u], 16)
                sp.dma_start(b2_row[u][:, :], b2p[:, ds(expert * D, D)]).then_inc(e_v[u], 16)
            blocks(sp, load)

            for u in range(SLOTS):
                sp.wait_ge(e_out[u], 32 * ((NBLK - u + SLOTS - 1) // SLOTS))
            ya_v = ys[0:N, :].rearrange("(t p) d -> p t d", p=P)
            yb_v = ys[N:2 * N, :].rearrange("(t p) d -> p t d", p=P)

            def fetch(g, u, i):
                at = ds(g * TILES, TILES)
                if later(g, 2):
                    wait_alone(sp, f_sum[u], i)
                sp.dma_start(ya[:, at, :], ya_v[:, at, :]).then_inc(f_in[u], 16)
                sp.dma_start(yb[:, at, :], yb_v[:, at, :]).then_inc(f_in[u], 16)
            pairs(sp, fetch)

        @block.gpsimd
        def _(pool):
            pool.memset(wfd[:, :], 0.0).then_inc(cleared, 1)
            pool.memset(x1[:, 0:2 * CH, :], 0.0).then_inc(cleared, 1)
            pool.memset(x1[:, 2 * CH:, :], 0.0).then_inc(bias_cleared, 1)
            pool.wait_ge(bias_cleared, 1)
            for r in (0, 32, 64):
                pool.dma_start(bias_raw[r:r + 1, 0:S].rearrange("p (h d) -> p h d", d=DH),
                               bf[None, None, :].broadcast_to([1, S // DH, DH])).then_inc(in_bias, 16)
                pool.dma_start(bias_raw[r:r + 1, S:], b2).then_inc(in_bias, 16)

            def scatter(b, prev, cur):
                if not prev:
                    return
                if isinstance(b, int) and b == 0:
                    return
                wait_alone(pool, route, ROUTE_STEPS * b)
                for j in range(TILES):
                    for k in range(TOPK):
                        pool.indirect_dma_start(xs, bass.IndirectOffsetOnAxis(ap=pos[:, j, k:k + 1], axis=0),
                                                rows[:, j, k, :], None).then_inc(scattered, 16)
            pool.wait_ge(filled, 16)
            batches(pool, scatter)

            def store(n, u, i):
                wait_alone(pool, e_y, n + 1)
                for c in range(2):
                    pool.indirect_dma_start(ys, bass.IndirectOffsetOnAxis(ap=xrow[u][:, c, D:D + 1].bitcast(I32), axis=0),
                                            yrow[u][:, c, :], None, bounds_check=TOPK * N - 1, oob_is_err=False).then_inc(e_out[u], 16)
            blocks(pool, store)

            def add(g, u, i):
                at = ds(g * TILES, TILES)
                pool.wait_ge(f_in[u], 32 * i + 32)
                pool.tensor_tensor(ya[:, at, :], ya[:, at, :], yb[:, at, :], ALU.add).then_inc(f_sum[u], 1)
            pairs(pool, add)

        @block.tensor
        def _(pe):
            mm = pe.matmul

            def three(outp, a_hi, a_lo, b_hi, b_lo, start=True, stop=True):
                mm(outp, a_hi, b_hi, start=start, stop=False)
                mm(outp, a_hi, b_lo, start=False, stop=False)
                return mm(outp, a_lo, b_hi, start=False, stop=stop)

            pe.wait_ge(in_fold, 80)
            for part in range(2):
                for c in range(CH):
                    last = mm(psA[:, part, c * P:(c + 1) * P], wqkvT_sb[:, part * CH + c, :], wfd[:, :], start=True, stop=True)
                last.then_inc(fold_pe, 1)
            for half in range(2):
                pe.wait_ge(fold_lo, half + 1)
                for c in range(CH // 2):
                    cc = half * CH // 2 + c
                    last = mm(psA[:, half, c * 256:(c + 1) * 256], wqkvT_sb[:, 2 * CH + cc, :], woutd[:, cc, :, :], start=True, stop=True)
                last.then_inc(fold_pe, 1)
            pe.wait_ge(in_c, 16)
            pe.wait_ge(in_small, 64)
            mm(psS[:, 0:E], con("ones"), gw[:, :], start=True, stop=True).then_inc(mean_pe, 1)
            pe.wait_ge(cast, 5)
            pe.wait_ge(bias_step, 9)
            pe.wait_ge(gwc_ready, 1)
            pe.wait_ge(fold_lo, 4)

            def attention(b, prev, cur):
                def turn_norms():
                    wait_alone(pe, n_step, N_STEPS * b)
                    for j in range(TILES):
                        last = pe.transpose(psS_r[:, j * P:(j + 1) * P], rparts[:, j, :, :].rearrange("p s h -> p (s h)"), ident_b[:, :])
                    last.then_inc(rT_pe, 1)

                def spread(c):
                    if c == 0:
                        pe.wait_ge(rT_done, b)
                        pe.wait_ge(g_l, 2 * b)
                    if c >= 2:
                        pe.wait_ge(qn_done, CH * (b - 1) + c - 1)
                    mm(psG[:, c % 2, :], sel_b[:, c, :], rT[:, :], start=True, stop=True).then_inc(bc_pe, 1)

                def output(c):
                    if c == 0:
                        pe.wait_ge(m_l, 2 * b)
                        pe.wait_ge(route, ROUTE_STEPS * (b - 1))
                    pe.wait_ge(qn_l, CH * (b - 1) + c + 1)
                    three(psO[:, :], m_hi[:, c, :], m_lo[:, c, :], qn_hi[:, c % 2, :], qn_lo[:, c % 2, :],
                          start=c == 0, stop=c == CH - 1).then_inc(o_pe, 1)

                def keys(t):
                    if t == 0:
                        pe.wait_ge(xT_l, b + 1)
                        pe.wait_ge(m_l, 2 * b)
                    if t >= 2:
                        pe.wait_ge(k_l, TILES * b + t - 1)
                    at = slice(t * P, (t + 1) * P)
                    for h in range(2):
                        to = psA[:, t % 2, h * 512:(h + 1) * 512]
                        cols = slice(h * 512, (h + 1) * 512)
                        mm(to, ones_b[0:65, :], parts[:, 0:S], start=True, stop=False)
                        mm(to, xT_hi[:, at], wk_hi[:, cols], start=False, stop=False)
                        mm(to, xT_hi[:, at], wk_lo[:, cols], start=False, stop=False)
                        last = mm(to, xT_lo[:, at], wk_hi[:, cols], start=False, stop=True)
                    last.then_inc(k_pe, 1)

                def queries(i):
                    if i < 2:
                        pe.wait_ge(k_l, TILES * b + i + 3)
                    else:
                        pe.wait_ge(q_done, CH // 2 * b + i - 1)
                    for j in range(2):
                        c = 2 * i + j
                        at = slice(c * P, (c + 1) * P)
                        last = three(psA[:, i % 2, j * 512:(j + 1) * 512], wq_hi[:, at], wq_lo[:, at], xT_hi[:, :], xT_lo[:, :])
                    last.then_inc(q_pe, 1)

                def logits():
                    pe.wait_ge(zT_done, b)
                    for j in range(TILES):
                        last = mm(psS_l[:, j, :], zT[:, j * P:(j + 1) * P], gwc[:, :], start=True, stop=True)
                    last.then_inc(l_pe, 1)
                    for j in range(TILES):
                        last = pe.transpose(psO_z[:, j, :], zT[:, j * P:(j + 1) * P], con("ident"))
                    last.then_inc(z_pe, 1)

                def ranks():
                    pe.wait_ge(x1_done, TILES * b)
                    pe.wait_ge(route, ROUTE_STEPS * (b - 1) + HOT_AT)
                    mm(psO_c[:, :, :], tri_b[:, :], hot_sum[:, :, :], start=True, stop=False)
                    for j in range(TILES):
                        last = mm(psO_c[:, j + 1:, :], ones_b[:, :], hot_sum[:, j:j + 1, :].broadcast_to([P, TILES - j, E]),
                                  start=False, stop=j == TILES - 1)
                    last.then_inc(c_pe, 1)

                def sums():
                    if not (isinstance(b, int) and b == 0):
                        pe.wait_ge(route, ROUTE_STEPS * (b - 1) + 1)
                    for c in range(CH):
                        for t in range(TILES):
                            for n, part in enumerate((k_hi, k_lo)):
                                last = mm(psS_k[:, c, :], part[:, t, c * P:(c + 1) * P], ones_r[:, :],
                                          start=t == 0 and n == 0, stop=t == TILES - 1 and n == 1)
                    last.then_inc(ks_pe, 1)

                def gram(h):
                    if h == 0:
                        pe.wait_ge(x_l, b + 1)
                        if not (isinstance(b, int) and b == 0):
                            pe.wait_ge(qn_done, CH * b)
                    cols = slice(h * 512, (h + 1) * 512)
                    for t in range(TILES):
                        last = three(psG[:, h, :], x_hi[:, t, :], x_lo[:, t, :], k_hi[:, t, cols], k_lo[:, t, cols],
                                     start=t == 0, stop=t == TILES - 1)
                    last.then_inc(g_pe, 1)

                def norms():
                    pe.wait_ge(ks_done, b + 1)
                    pe.wait_ge(q_done, CH // 2 * (b + 1))
                    for j in range(TILES):
                        for c in range(CH):
                            last = mm(psS_n[:, j, :], q_act[:, c, j * P:(j + 1) * P], ksd[:, c, :], start=c == 0, stop=c == CH - 1)
                    last.then_inc(n_pe, 1)

                def mix(half):
                    pe.wait_ge(g_l, 2 * b + half + 1)
                    for i in range(CH // 2):
                        c = half * CH // 2 + i
                        at, cols = slice(c * P, (c + 1) * P), slice(2 * c * D, 2 * (c + 1) * D)
                        last = three(psA[:, half, i * 256:(i + 1) * 256], g_hi[:, at], g_lo[:, at], vo_hi[:, cols], vo_lo[:, cols])
                    last.then_inc(m_pe, 1)

                if prev:
                    turn_norms()
                    spread(0)
                    spread(1)
                if cur:
                    keys(0)
                for t in range(TILES):
                    if prev:
                        output(2 * t)
                        if 2 * t + 2 < CH:
                            spread(2 * t + 2)
                        output(2 * t + 1)
                        if 2 * t + 3 < CH:
                            spread(2 * t + 3)
                    if cur and t + 1 < TILES:
                        keys(t + 1)
                if cur:
                    queries(0)
                if prev:
                    logits()
                if cur:
                    for i in range(1, CH // 2):
                        queries(i)
                    sums()
                    gram(0)
                if prev:
                    ranks()
                if cur:
                    gram(1)
                    norms()
                    mix(0)
                    mix(1)
            batches(pe, attention)

            def turn_rows(n, u, i):
                pe.wait_ge(e_x[u], 16 * i + 16)
                if later(n, 2):
                    pe.wait_ge(e_Tl, n - 1)
                for c in range(2):
                    last = pe.transpose(psX[u % 2][:, c * P:(c + 1) * P], xrow[u][:, c, 0:D], con("ident"))
                last.then_inc(e_T, 1)

            def first_layer(n, u, i):
                v = u % 2
                pe.wait_ge(e_Tl, n + 1)
                pe.wait_ge(e_wl, n + 1)
                if later(n, 2):
                    pe.wait_ge(e_gelu, FC * (n - 1))
                at = slice(v * BLK, (v + 1) * BLK)
                for c in range(FC):
                    w = slice(v * F + c * P, v * F + (c + 1) * P)
                    last = three(psH[v][:, c, :], wq_hi[:, w], wq_lo[:, w], xT_hi[:, at], xT_lo[:, at])
                    last.then_inc(e_up, 1)

            def second_layer(n, u, i):
                v = u % 2
                pe.wait_ge(e_v[u], 32 * i + 32)
                pe.wait_ge(e_gelu, FC * (n + 1))
                if later(n, 2):
                    pe.wait_ge(e_y, n - 1)
                for t in range(2):
                    mm(psY[v][:, t, :], ones_b[0:3, :], b2_row[u][:, :], start=True, stop=False)
                    for c in range(FC):
                        last = mm(psY[v][:, t, :], hT[v][:, c, t * P:(t + 1) * P], w2_raw[u][:, c, :], start=False, stop=c == FC - 1)
                last.then_inc(e_down, 1)

            def experts(n, u, i):
                turn_rows(n, u, i)
                if later(n, 1):
                    first_layer(*earlier(n, u, i, 1))
                if later(n, 2):
                    second_layer(*earlier(n, u, i, 2))
            blocks(pe, experts)
            first_layer(*last_blocks[1])
            second_layer(*last_blocks[0])
            second_layer(*last_blocks[1])

        @block.scalar
        def _(act):
            def hi(out_, in_, func=ACT.Copy, **kw):
                return act.activation(out_, in_, func, **kw)

            act.dma_start(cst[:, :], consts).then_inc(in_c, 16)
            act.dma_start(gw[:, :], gwT).then_inc(in_small, 16)
            act.dma_start(bout_col[:, :], bout.rearrange("(d a) -> d a", a=1)).then_inc(in_small, 16)
            act.dma_start(bf_col[0:DH, :], bf.rearrange("(d a) -> d a", a=1)).then_inc(in_small, 16)
            act.dma_start(bf_col[DH:P, :], bf.rearrange("(d a) -> d a", a=1)).then_inc(in_small, 16)
            folded = [(wq_hi[:, :], 0), (wk_hi[:, :], 1), (vo_hi[:, 0:1024], 0), (vo_hi[:, 1024:], 1)]
            for i, (to, half) in enumerate(folded):
                act.wait_ge(fold_pe, i + 1)
                hi(to, psA[:, half, :]).then_inc(fold_hi, 1)

            def attention(b, prev, cur):
                def out_hi(c):
                    act.wait_ge(qn_done, CH * (b - 1) + c + 1)
                    act.wait_ge(o_pe, CH * (b - 1) + max(c - 1, 0))
                    hi(qn_hi[:, c % 2, :], qn[:, c % 2, :]).then_inc(qn_h, 1)

                def key_hi(t):
                    act.wait_ge(k_pe, TILES * b + t + 1)
                    if t == 0:
                        act.wait_ge(g_pe, 2 * b)
                        act.wait_ge(ks_pe, b)
                    hi(k_hi[:, t, :], psA[:, t % 2, :], ACT.Relu).then_inc(k_h, 1)

                def query(i):
                    act.wait_ge(q_pe, CH // 2 * b + i + 1)
                    if i == 0:
                        act.wait_ge(n_pe, b)
                        act.wait_ge(qn_done, CH * b)
                    hi(q_act[:, 2 * i:2 * i + 2, :], psA[:, i % 2, :].rearrange("p (c s) -> p c s", c=2), ACT.Relu,
                       bias=bf_col[:, 0:1]).then_inc(q_done, 1)

                if cur:
                    if isinstance(b, int) and b == 0:
                        act.wait_ge(in_x0, 32)
                    else:
                        act.wait_ge(in_x, 32)
                    act.wait_ge(q_pe, CH // 2 * b)
                    hi(xT_hi[:, :], xT_raw[:, ds(b * S, S)]).then_inc(xT_h, 1)
                if prev:
                    act.wait_ge(rT_pe, b)
                    hi(rT[:, :], psS_r).then_inc(rT_done, 1)
                for t in range(TILES):
                    if prev:
                        out_hi(2 * t)
                    if cur:
                        key_hi(t)
                    if prev:
                        out_hi(2 * t + 1)
                if cur:
                    act.wait_ge(g_pe, 2 * b)
                    hi(x_hi[:, :, :], x_raw[:, ds(b * TILES, TILES), :]).then_inc(x_h, 1)
                    query(0)
                    query(1)
                if prev:
                    act.wait_ge(ln_step, LN_STEPS * b)
                    for j in range(TILES):
                        act.activation(x1[:, ds((b - 1) * TILES + j, 1), :], psO_z[:, j:j + 1, :], ACT.Identity,
                                       bias=ln[:, 3, j:j + 1], scale=ln[:, 1, j:j + 1]).then_inc(x1_done, 1)
                if cur:
                    query(2)
                if prev:
                    act.wait_ge(route, ROUTE_STEPS * (b - 1) + TOP_AT)
                    act.activation(tope[:, :, :], topd[:, :, :], ACT.Exp).then_inc(exp_done, 1)
                if cur:
                    query(3)
                    for h in range(2):
                        act.wait_ge(g_pe, 2 * b + h + 1)
                        if h == 0:
                            act.wait_ge(m_pe, 2 * b)
                        hi(g_hi[:, h * 512:(h + 1) * 512], psG[:, h, :]).then_inc(g_h, 1)
                    for h in range(2):
                        act.wait_ge(m_pe, 2 * b + h + 1)
                        if h == 0:
                            act.wait_ge(o_pe, CH * b)
                        m_v = psA[:, h, :].rearrange("p (c a d) -> p c a d", c=CH // 2, a=2)
                        for a in range(2):
                            r = slice(DH * a, DH * (a + 1))
                            hi(m_hi[r, h * CH // 2:(h + 1) * CH // 2, :], m_v[r, :, a, :]).then_inc(m_h, 1)
            batches(act, attention)

            def gelu(n, u, i):
                v = u % 2
                act.wait_ge(e_w[u], 16 * i + 16)
                for c in range(FC):
                    act.wait_ge(e_up, FC * n + c // 2 * 2 + 2)
                    if c == 0 and later(n, 2):
                        act.wait_ge(e_down, n - 1)
                    act.activation(hT[v][:, c, :], psH[v][:, c, :], ACT.Gelu_apprx_tanh,
                                   bias=w1_raw[u][:, F + c:F + c + 1]).then_inc(e_gelu, 1)

            def experts(n, u, i):
                act.wait_ge(e_T, n + 1)
                if later(n, 2):
                    act.wait_ge(e_up, FC * (n - 1))
                v = u % 2
                hi(xT_hi[:, v * BLK:(v + 1) * BLK], psX[v]).then_inc(e_Th, 1)
                if later(n, 1):
                    gelu(*earlier(n, u, i, 1))
            blocks(act, experts)
            gelu(*last_blocks[1])

            out_v = out.rearrange("b (t p) d -> p (b t) d", p=P)

            def finish(g, u, i):
                act.wait_ge(f_ln, LN_STEPS * (g + 1))
                for j in range(TILES):
                    at = ds(g * TILES + j, 1)
                    act.activation(yb[:, at, :], x1[:, at, :], ACT.Identity,
                                   bias=ln[:, 3, j:j + 1], scale=ln[:, 1, j:j + 1]).then_inc(f_norm, 1)
                act.wait_ge(f_norm, TILES * (g + 1))
                act.dma_start(out_v[:, ds(g * TILES, TILES), :], yb[:, ds(g * TILES, TILES), :]).then_inc(f_out[u], 16)
            pairs(act, finish)
            for u in range(2):
                act.wait_ge(f_out[u], 16 * B // 2)

        @block.vector
        def _(dve):
            def lo(out_, full_, hi_):
                return dve.tensor_tensor(out_, full_, hi_.bitcast(F32), ALU.subtract)

            def norm_steps(step):
                v, y, t, nb = (ln[:, i, :] for i in range(4))
                step(dve.tensor_scalar(v, mv[:, :, 1], LN_EPS, None, ALU.add))
                step.wait()
                step(dve.tensor_scalar(y.bitcast(I32), v.bitcast(I32), -0.5, RSQRT_SEED, ALU.mult, ALU.add))
                for _ in range(3):
                    step.wait()
                    step(dve.tensor_tensor(t, v, y, ALU.mult))
                    step.wait()
                    step(dve.tensor_tensor(t, t, y, ALU.mult))
                    step.wait()
                    step(dve.tensor_scalar(t, t, -0.5, 1.5, ALU.mult, ALU.add))
                    step.wait()
                    step(dve.tensor_tensor(y, y, t, ALU.mult))
                step.wait()
                step(dve.scalar_tensor_tensor(nb, mv[:, :, 0], -1.0, y, ALU.mult, ALU.mult))

            dve.memset(zeros[:, :, :], 0.0).then_inc(zero_ready, 1)
            dve.wait_ge(zero_ready, 1)
            dve.memset(zeros[:, :, D:D + 1].bitcast(I32), 65535).then_inc(zero_ready, 1)
            dve.memset(rows[:, :, :, :], 0.0).then_inc(cast, 1)
            dve.memset(hot_sum[:, :, :], 0.0).then_inc(cast, 1)
            dve.memset(parts[:, :], 0.0).then_inc(cast, 1)
            dve.wait_ge(in_c, 16)
            dve.tensor_copy(ones_r[:, :], con("ones")[:, 0:2]).then_inc(cast, 1)
            dve.tensor_copy(ones_b[:, :], con("ones")).then_inc(cast, 1)
            dve.tensor_copy(tri_b[:, :], con("tri")).then_inc(cast, 1)
            dve.tensor_copy(ident_b[:, :], con("ident")).then_inc(cast, 1)
            dve.tensor_copy(sel_b[:, :, :], con("sel", 3 * H).rearrange("p (c m) -> p c m", c=CH)).then_inc(cast, 1)
            dve.tensor_copy(base[:, :], con("first")).then_inc(cast, 1)
            dve.tensor_copy(dest[:, :, :], con("dest").rearrange("p (t k) -> p t k", k=TOPK)).then_inc(cast, 1)
            dve.wait_ge(in_bias, 96)
            dve.wait_ge(cast, 10)
            step = Steps(dve, bias_step, 0)
            for i, r in enumerate((0, 32, 64)):
                step(dve.tensor_copy(bias_part, bias_raw))
                step.wait()
                step(dve.tensor_copy(parts[r:r + 1, :], bias_part[r:r + 1, :]))
                step(dve.tensor_tensor(bias_raw, bias_raw, bias_part, ALU.subtract))
                step.wait()
            folded = [(wq_hi[:, :], wq_lo[:, :], 0), (wk_hi[:, :], wk_lo[:, :], 1),
                      (vo_hi[:, 0:1024], vo_lo[:, 0:1024], 0), (vo_hi[:, 1024:], vo_lo[:, 1024:], 1)]
            for i, (h_, l_, half) in enumerate(folded):
                dve.wait_ge(fold_hi, i + 1)
                lo(l_, psA[:, half, :], h_).then_inc(fold_lo, 1)
            dve.wait_ge(mean_pe, 1)
            dve.wait_ge(in_small, 64)
            dve.scalar_tensor_tensor(gwc[:, :], psS[:, 0:E], -1.0 / D, gw[:, :], ALU.mult, ALU.add).then_inc(gwc_ready, 1)

            def attention(b, prev, cur):
                def normalise(c):
                    dve.wait_ge(bc_pe, CH * (b - 1) + c + 1)
                    dve.wait_ge(qn_l, CH * (b - 1) + max(c - 1, 0))
                    dve.tensor_tensor(qn[:, c % 2, :], q_act[:, c, :], psG[:, c % 2, :], ALU.mult).then_inc(qn_done, 1)

                def out_lo(c):
                    dve.wait_ge(qn_h, CH * (b - 1) + c + 1)
                    lo(qn_lo[:, c % 2, :], qn[:, c % 2, :], qn_hi[:, c % 2, :]).then_inc(qn_l, 1)

                def key_lo(t):
                    dve.wait_ge(k_h, TILES * b + t + 1)
                    dve.scalar_tensor_tensor(k_lo[:, t, :], psA[:, t % 2, :], 0.0, k_hi[:, t, :].bitcast(F32),
                                             ALU.max, ALU.subtract).then_inc(k_l, 1)

                step = Steps(dve, route, ROUTE_STEPS * (b - 1))

                def choose():
                    dve.wait_ge(l_pe, b)
                    step(dve.tensor_tensor(logit[:, :, :], psS_l, ln[:, 1, :][:, :, None].broadcast_to([P, TILES, E]), ALU.mult))
                    wait_alone(dve, step.which, step.n)
                    for j in range(TILES):
                        step(dve.max(top[:, j, :], logit[:, j, :]))
                    wait_alone(dve, step.which, step.n)
                    for j in range(TILES):
                        step(dve.max_index(topi[:, j, :], top[:, j, :], logit[:, j, :]))
                    step(dve.tensor_tensor(topd[:, :, :], top[:, :, :], top[:, :, 0:1].broadcast_to([P, TILES, 8]), ALU.subtract))
                    step.wait()
                    step(dve.tensor_copy(topf[:, :, :], topi[:, :, 0:TOPK]))
                    step.wait()
                    step(dve.tensor_tensor(hot[:, :, :, :].rearrange("p t k e -> p (t k) e"),
                                           con("iota")[:, None, :].broadcast_to([P, TILES * TOPK, E]),
                                           topf[:, :, :].rearrange("p t k -> p (t k)")[:, :, None].broadcast_to([P, TILES * TOPK, E]),
                                           ALU.is_equal))
                    step.wait()
                    step(dve.tensor_tensor(hot_sum[:, 0:TILES, :], hot[:, :, 0, :], hot[:, :, 1, :], ALU.add))
                    dve.wait_ge(exp_done, b)
                    step(dve.tensor_reduce(den[:, 0, :], tope[:, :, :], AX_X, ALU.add))
                    step.wait()
                    step(dve.reciprocal(den[:, 1, :], den[:, 0, :]))
                    step.wait()
                    dve.wait_ge(scattered, 16 * TILES * TOPK * (b - 1))
                    step(dve.tensor_tensor(rows[:, :, :, D + 1], tope[:, :, 0:TOPK],
                                           den[:, 1, :][:, :, None].broadcast_to([P, TILES, TOPK]), ALU.mult))
                    step(dve.tensor_copy(rows[:, :, :, D].bitcast(I32), dest[:, :, :]))
                    step.wait()
                    step(dve.tensor_scalar(dest[:, :, :], dest[:, :, :], float(S), None, ALU.add))
                    dve.wait_ge(x1_done, TILES * b)
                    step(dve.tensor_copy(rows[:, :, :, 0:D],
                                         x1[:, ds((b - 1) * TILES, TILES), :][:, :, None, :].broadcast_to([P, TILES, TOPK, D])))

                def place():
                    dve.wait_ge(c_pe, b)
                    step(dve.tensor_tensor(rank[:, :, :], psO_c[:, 0:TILES, :], base[:, None, :].broadcast_to([P, TILES, E]), ALU.add))
                    step.wait()
                    step(dve.tensor_tensor(base[:, :], base[:, :], psO_c[:, TILES, :], ALU.add))
                    step(dve.tensor_tensor(picked[:, :, :, :], hot[:, :, :, :],
                                           rank[:, :, None, :].broadcast_to([P, TILES, TOPK, E]), ALU.mult))
                    step.wait()
                    step(dve.tensor_reduce(posf[:, :, :], picked[:, :, :, :], AX_X, ALU.add))
                    step.wait()
                    step(dve.tensor_copy(pos[:, :, :], posf[:, :, :]))

                if cur:
                    dve.wait_ge(xT_h, b + 1)
                    lo(xT_lo[:, :], xT_raw[:, ds(b * S, S)], xT_hi[:, :]).then_inc(xT_l, 1)
                if prev:
                    normalise(0)
                for t in range(TILES):
                    if prev:
                        normalise(2 * t + 1)
                        out_lo(2 * t)
                    if cur:
                        key_lo(t)
                    if prev:
                        out_lo(2 * t + 1)
                        if 2 * t + 2 < CH:
                            normalise(2 * t + 2)
                if prev:
                    dve.wait_ge(o_pe, CH * b)
                    dve.scalar_tensor_tensor(zT[:, :], psO[:, :], bout_col[:, 0:1], xT_raw[:, ds((b - 1) * S, S)],
                                             ALU.add, ALU.add).then_inc(zT_done, 1)
                if cur:
                    dve.wait_ge(x_h, b + 1)
                    lo(x_lo[:, :, :], x_raw[:, ds(b * TILES, TILES), :], x_hi[:, :, :]).then_inc(x_l, 1)
                if prev:
                    dve.wait_ge(z_pe, b)
                    st = Steps(dve, st_step, ST_STEPS * (b - 1))
                    for j in range(TILES):
                        st(dve.bn_stats(stats[:, j, :], psO_z[:, j, :]))
                    wait_alone(dve, st.which, st.n)
                    for j in range(TILES):
                        st(dve.bn_aggr(mv[:, j, :], stats[:, j, :]))
                    st.wait()
                    norm_steps(Steps(dve, ln_step, LN_STEPS * (b - 1)))
                    dve.wait_ge(ln_step, LN_STEPS * b)
                    choose()
                if cur:
                    dve.wait_ge(ks_pe, b + 1)
                    dve.wait_ge(n_pe, b)
                    dve.tensor_tensor(ksd[:, :, :], con("mask").rearrange("p (c h) -> p c h", h=H),
                                      psS_k[:, :, 0:1].broadcast_to([P, CH, H]), ALU.mult).then_inc(ks_done, 1)
                    for h in range(2):
                        cols = slice(h * 512, (h + 1) * 512)
                        dve.wait_ge(g_h, 2 * b + h + 1)
                        lo(g_lo[:, cols], psG[:, h, :], g_hi[:, cols]).then_inc(g_l, 1)
                if prev:
                    place()
                if cur:
                    dve.wait_ge(n_pe, b + 1)
                    ns = Steps(dve, n_step, N_STEPS * b)
                    ns(dve.tensor_scalar(rn[:, 0, :, :], psS_n, NORM_EPS, None, ALU.add))
                    ns.wait()
                    ns(dve.reciprocal(rn[:, 1, :, :], rn[:, 0, :, :]))
                    ns.wait()
                    ns(dve.tensor_copy(rparts[:, :, 0, :], rn[:, 1, :, :]))
                    ns.wait()
                    ns(dve.tensor_tensor(rn[:, 2, :, :], rn[:, 1, :, :], rparts[:, :, 0, :], ALU.subtract))
                    ns.wait()
                    ns(dve.tensor_copy(rparts[:, :, 1, :], rn[:, 2, :, :]))
                    ns.wait()
                    ns(dve.tensor_tensor(rparts[:, :, 2, :], rn[:, 2, :, :], rparts[:, :, 1, :], ALU.subtract))
                    for h in range(2):
                        m_v = psA[:, h, :].rearrange("p (c a d) -> p c a d", c=CH // 2, a=2)
                        dve.wait_ge(m_h, 4 * b + 2 * h + 2)
                        for a in range(2):
                            r, cs = slice(DH * a, DH * (a + 1)), slice(h * CH // 2, (h + 1) * CH // 2)
                            ins = lo(m_lo[r, cs, :], m_v[r, :, a, :], m_hi[r, cs, :])
                            if a == 1:
                                ins.then_inc(m_l, 1)
                            else:
                                ins.then_inc(m_l0, 1)
            batches(dve, attention)

            first_ = con("first", 1)
            dve.wait_ge(route, ROUTE_STEPS * B)
            tb = Steps(dve, tab_step, 0)
            tb(dve.tensor_tensor(cnt[:, 0, :], base[0:1, :], first_, ALU.subtract))
            tb.wait()
            tb(dve.tensor_tensor(full[:, :, :], cnt[:, 0, :][:, :, None].broadcast_to([1, E, 16]),
                                 con("step", 1).rearrange("p (e s) -> p e s", e=E), ALU.is_gt))
            tb.wait()
            tb(dve.tensor_reduce(cnt[:, 1, :], full[:, :, :], AX_X, ALU.add))
            tb.wait()
            tb(dve.tensor_tensor(upto_n[:, :, :], con("upto", 1).rearrange("p (a e) -> p a e", a=E),
                                 cnt[:, 1:2, :].broadcast_to([1, E, E]), ALU.mult))
            tb.wait()
            tb(dve.tensor_reduce(cnt[:, 2, :], upto_n[:, :, :], AX_X, ALU.add))
            tb.wait()
            tb(dve.tensor_tensor(past[:, 0, :, :], cnt[:, 2:3, :].broadcast_to([1, NBLK, E]),
                                 con("block", 1)[:, :, None].broadcast_to([1, NBLK, E]), ALU.is_le))
            tb.wait()
            tb(dve.tensor_reduce(tab[:, 0, :], past[:, 0, :, :], AX_X, ALU.add))
            tb(dve.tensor_tensor(past[:, 1, :, :], past[:, 0, :, :], cnt[:, 1:2, :].broadcast_to([1, NBLK, E]), ALU.mult))
            tb.wait()
            tb(dve.tensor_reduce(tab[:, 1, :], past[:, 1, :, :], AX_X, ALU.add))
            tb.wait()
            tb(dve.tensor_tensor(tab[:, 2, :], con("block", 1), tab[:, 1, :], ALU.subtract))
            tb.wait()
            tb(dve.tensor_scalar(tab[:, 3, :], tab[:, 2, :], float(BLK), None, ALU.mult))
            tb.wait()
            tb(dve.scalar_tensor_tensor(tab[:, 4, :], tab[:, 0, :], float(REGION), tab[:, 3, :], ALU.mult, ALU.add))
            tb.wait()
            dve.tensor_scalar(tabi[:, 0, :], tab[:, 0, :], float(E - 1), None, ALU.min).then_inc(table, 1)
            dve.tensor_scalar(tabi[:, 1, :], tab[:, 4, :], float(NOWHERE), None, ALU.min).then_inc(table, 1)

            def result(n, u, i):
                v = u % 2
                dve.wait_ge(e_down, n + 1)
                if later(n, SLOTS):
                    dve.wait_ge(e_out[u], 32 * i)
                dve.tensor_scalar(yrow[u][:, 0, :], psY[v][:, 0, :], xrow[u][:, 0, D + 1:D + 2], None, ALU.mult).then_inc(e_y0, 1)
                dve.tensor_scalar(yrow[u][:, 1, :], psY[v][:, 1, :], xrow[u][:, 1, D + 1:D + 2], None, ALU.mult).then_inc(e_y, 1)

            def experts(n, u, i):
                v = u % 2
                at, ws = slice(v * BLK, (v + 1) * BLK), slice(v * F, (v + 1) * F)
                dve.wait_ge(e_w[u], 16 * i + 16)
                if later(n, 2):
                    dve.wait_ge(e_up, FC * (n - 1))
                dve.tensor_copy(wq_hi[:, ws], w1_raw[u][:, 0:F]).then_inc(e_wh, 1)
                dve.wait_ge(e_wh, n + 1)
                lo(wq_lo[:, ws], w1_raw[u][:, 0:F], wq_hi[:, ws]).then_inc(e_wl, 1)
                dve.wait_ge(e_Th, n + 1)
                lo(xT_lo[:, at], psX[v], xT_hi[:, at]).then_inc(e_Tl, 1)
                if later(n, 2):
                    result(*earlier(n, u, i, 2))
            blocks(dve, experts)
            result(*last_blocks[0])
            result(*last_blocks[1])


            def normalise_sum(g, u, i):
                at = ds(g * TILES, TILES)
                dve.wait_ge(f_sum[u], i + 1)
                dve.tensor_tensor(x1[:, at, :], x1[:, at, :], ya[:, at, :], ALU.add).then_inc(f_z, 1)
                wait_alone(dve, f_z, g + 1)
                st = Steps(dve, f_stats, ST_STEPS * g)
                for j in range(TILES):
                    st(dve.bn_stats(stats[:, j, :], x1[:, ds(g * TILES + j, 1), :].rearrange("p a d -> p (a d)")))
                wait_alone(dve, st.which, st.n)
                for j in range(TILES):
                    st(dve.bn_aggr(mv[:, j, :], stats[:, j, :]))
                st.wait()
                if later(g, 1):
                    dve.wait_ge(f_norm, TILES * g)
                norm_steps(Steps(dve, f_ln, LN_STEPS * g))
            pairs(dve, normalise_sum)


def kernel(L0_attn_x, L0_attn_W_qkv, L0_attn_W_f, L0_attn_b_f, L0_attn_W_out, L0_attn_b_out,
           L0_ffn_gate_w, L0_ffn_w1, L0_ffn_b1, L0_ffn_w2, L0_ffn_b2):
    import concourse.bacc as bacc
    from concourse.bass_utils import run_bass_kernel_spmd

    def f(a):
        return np.ascontiguousarray(a)
    x = np.asarray(L0_attn_x).reshape(N, D)
    w1 = np.transpose(np.asarray(L0_ffn_w1), (1, 2, 0))
    b1 = np.transpose(np.asarray(L0_ffn_b1).reshape(E, FC, P), (0, 2, 1))
    w2 = np.transpose(np.asarray(L0_ffn_w2).reshape(D, E, FC, P), (1, 3, 2, 0)).reshape(E, P, FC * D)
    arrays = {
        "x": f(x), "xT": f(x.T), "wqkvT": f(np.asarray(L0_attn_W_qkv).T), "wf": f(L0_attn_W_f), "bf": f(L0_attn_b_f),
        "wout": f(L0_attn_W_out), "bout": f(L0_attn_b_out), "gwT": f(np.asarray(L0_ffn_gate_w).T),
        "w1": f(np.concatenate([w1, b1], axis=2)), "w2": f(w2), "b2": f(np.asarray(L0_ffn_b2).reshape(1, E * D)),
        "consts": shape_constants(),
    }
    nc = bacc.Bacc("TRN2", target_bir_lowering=False, num_devices=1)
    args = {n: nc.dram_tensor(n, a.shape, mybir.dt.from_np(a.dtype), kind="ExternalInput").ap() for n, a in arrays.items()}
    out = nc.dram_tensor("out", (B, S, D), F32, kind="ExternalOutput").ap()
    program(nc, out=out, **args)
    r = run_bass_kernel_spmd(nc, [arrays], core_ids=[0])
    return r.results[0]["out"]
```

```python
from contextlib import ExitStack

import numpy as np

import concourse.bass as bass
from concourse import mybir

ALU = mybir.AluOpType
ACT = mybir.ActivationFunctionType
AX_X = mybir.AxisListType.X
F32 = mybir.dt.float32
F32R = mybir.dt.float32r
BF16 = mybir.dt.bfloat16
I32 = mybir.dt.int32
U32 = mybir.dt.uint32
ds = bass.ds

P = 128
D = 128
B, S = 8, 512
N = B * S
TILES = S // P
H, DH = 16, 64
HD = H * DH
CH = HD // P
E, F = 8, 512
FC = F // P
TOPK = 2
BLK = 256
NBLK = (N * TOPK + E * (BLK - 1)) // BLK
REGION = N + BLK
ROW = D + 4
FILL = 4
XS_ROWS = E * REGION + 1024
NOWHERE = E * REGION
LN_EPS = 1e-5
NORM_EPS = 1e-6
RSQRT_SEED = float(0x5F3759DF)
SLOTS = 6
PARTS_AT = (0, 4, 6)
W1_ROW = F + FC

_C = {}
_at = 0
for _name, _n in (("ident", P), ("tri", P), ("ones", P), ("mask", CH * H), ("iota", E), ("dest", TILES * TOPK),
                  ("first", E), ("block", NBLK), ("step", E * 16), ("upto", E * E),
                  ("sel", CH * P)):
    _C[_name] = (_at, _at + _n)
    _at += _n
C_COLS = _at
C_KEPT = _C["sel"][0]


def shape_constants():
    c = np.zeros((P, C_COLS), np.float32)

    def put(name, value):
        lo, hi = _C[name]
        value = np.asarray(value, np.float32).reshape(-1, hi - lo)
        c[:len(value) if len(value) > 1 else P, lo:hi] = value
    p = np.arange(P)
    put("ident", np.eye(P))
    put("tri", p[:, None] < p[None, :])
    put("ones", np.ones((P, P)))
    put("mask", (p[:, None, None] // DH + 2 * np.arange(CH)[None, :, None] == np.arange(H)[None, None, :]))
    put("iota", np.arange(E)[None])
    put("dest", p[:, None, None] + P * np.arange(TILES)[None, :, None] + N * np.arange(TOPK)[None, None, :])
    put("first", (REGION * np.arange(E))[None])
    put("sel", (p[:, None, None] % H == 2 * np.arange(CH)[None, :, None] + p[None, None, :] // DH)
        & np.isin(p // H, PARTS_AT)[:, None, None])
    put("block", np.arange(NBLK)[None])
    put("step", np.broadcast_to(BLK * np.arange(16)[None, :], (E, 16)).reshape(1, -1))
    put("upto", (np.arange(E)[None, :] <= np.arange(E)[:, None]).reshape(1, -1))
    return c



def program(nc, x, xT, wqkvT, wf, bf, wout, bout, gwT, w1, w2, b2, consts, out):
    ctx = ExitStack()
    with ctx:
        def sb(name, shape, dt=F32):
            return ctx.enter_context(nc.sbuf_tensor(name, shape, dt))

        def pb(name, shape, dt=F32):
            return ctx.enter_context(nc.psum_tensor(name, shape, dt))

        def sem(name):
            return ctx.enter_context(nc.semaphore(name))

        xs = nc.dram_tensor("expert_rows", [XS_ROWS, ROW], F32, kind="Internal").ap()
        ys = nc.dram_tensor("expert_results", [TOPK * N, D], F32, kind="Internal").ap()
        b2p = nc.dram_tensor("b2_parts", [3, S + E * D], BF16, kind="Internal").ap()

        cst = sb("cst", [P, C_KEPT])

        def con(name, rows=P):
            lo, hi = _C[name]
            return cst[0:rows, lo:hi]
        x_raw = sb("x_raw", [P, B * TILES, D])
        xT_raw = sb("xT_raw", [P, N + S])
        x1 = sb("x1", [P, B * TILES, D])
        wq_hi, wq_lo = sb("wq_hi", [P, HD], F32R), sb("wq_lo", [P, HD], F32R)
        wk_hi, wk_lo = sb("wk_hi", [P, HD], F32R), sb("wk_lo", [P, HD], F32R)
        vo_hi, vo_lo = sb("vo_hi", [P, H * D], F32R), sb("vo_lo", [P, H * D], F32R)
        xT_hi, xT_lo = sb("xT_hi", [P, S], F32R), sb("xT_lo", [P, S], F32R)
        x_hi, x_lo = sb("x_hi", [P, TILES, D], F32R), sb("x_lo", [P, TILES, D], F32R)
        k_hi, k_lo = sb("k_hi", [P, TILES, HD], F32R), sb("k_lo", [P, TILES, HD], F32R)
        q_act = sb("q_act", [P, CH, S])
        g_hi, g_lo = sb("g_hi", [P, CH, 2, 2, DH], F32R), sb("g_lo", [P, CH, 2, 2, DH], F32R)
        m_hi, m_lo = sb("m_hi", [P, CH, D], F32R), sb("m_lo", [P, CH, D], F32R)
        qn = sb("qn", [P, 4, S])
        qn_hi, qn_lo = sb("qn_hi", [P, 2, S], F32R), sb("qn_lo", [P, 2, S], F32R)
        rows = sb("rows", [P, TILES, TOPK, ROW])
        zeros = sb("zeros", [P, FILL, ROW])
        wfd = sb("wfd", [P, P])
        bf_col = sb("bf_col", [P, 1])
        bout_col = sb("bout_col", [P, 1])
        gw = sb("gw", [P, E])
        gwc = sb("gwc", [P, E])
        ones_r = sb("ones_r", [P, H], F32R)
        ones_b = sb("ones_b", [P, P], BF16)
        tri_b = sb("tri_b", [P, P], BF16)
        sel_b = sb("sel_b", [P, CH, P], BF16)
        bf_rows = sb("bf_rows", [3, S], BF16)
        ksd = sb("ksd", [P, CH, P // H, H])
        rn = sb("rn", [P, 2, S])
        rT = sb("rT", [P, S], BF16)
        stats = sb("stats", [P, 4 * TILES, 6])
        mv = sb("mv", [P, 4 * TILES, 2])
        ln = sb("ln", [P, 4, 4 * TILES])
        logit = sb("logit", [P, TILES, E])
        top = sb("top", [P, TILES, 8])
        topi = sb("topi", [P, TILES, 8], U32)
        topd = sb("topd", [P, TILES, 8])
        tope = sb("tope", [P, TILES, 8])
        den = sb("den", [P, 2, TILES])
        topf = sb("topf", [P, TILES, TOPK])
        hot = sb("hot", [P, TILES, TOPK, E])
        hot_sum = sb("hot_sum", [P, TILES + 1, E], BF16)
        rank = sb("rank", [P, TILES, E])
        picked = sb("picked", [P, TILES, TOPK, E])
        posf = sb("posf", [P, TILES, TOPK])
        pos = sb("pos", [P, TILES, TOPK], I32)
        base = sb("base", [P, E])
        dest = sb("dest", [P, TILES, TOPK])
        cnt = sb("cnt", [1, 3, E])
        full = sb("full", [1, E, 16])
        upto_n = sb("upto_n", [1, E, E])
        tab = sb("tab", [1, 5, NBLK])
        tabi = sb("tabi", [1, 2, NBLK], I32)
        wqkvT_sb = q_act[:, :, :].rearrange("p c s -> p (c s)")[:, 0:3 * HD].rearrange("p (c d) -> p c d", d=D)
        q_space = q_act[:, :, :].rearrange("p c s -> p (c s)")
        sel_f = q_space[:, 3 * HD:3 * HD + CH * P]
        woutd = x1[:, 0:2 * CH, :].rearrange("p (c a) d -> p c a d", a=2)
        bias_raw = x1[0:1, 2 * CH:2 * CH + (S + E * D) // D, :].rearrange("p c d -> p (c d)")
        zT = qn[:, 3, :]
        krow = qn[0:1, 1:3, :].rearrange("p a s -> p (a s)")
        bias_row = [t.bitcast(BF16)[:, 0:S + E * D] for t in (
            krow[:, :], ksd[0:1, :, :, :].rearrange("p c r h -> p (c r h)"), rn[0:1, :, :].rearrange("p a s -> p (a s)"))]
        past = krow[:, 0:2 * NBLK * E].rearrange("p (a n e) -> p a n e", a=2, e=E)
        b2_row = [zT[0:3, :].bitcast(BF16)[:, u * D:(u + 1) * D] for u in range(SLOTS)]
        hT = [q_space[:, v * FC * BLK:(v + 1) * FC * BLK].rearrange("p (c s) -> p c s", c=FC) for v in range(2)]
        yrow = [q_space[:, 2 * FC * BLK + 2 * u * D:2 * FC * BLK + 2 * (u + 1) * D].rearrange("p (c d) -> p c d", d=D) for u in range(SLOTS)]
        w1_raw = [xT_raw[:, u * W1_ROW:(u + 1) * W1_ROW] for u in range(SLOTS)]
        xrow = [rows[:, u, :, :] for u in range(TILES)] + [
            x_raw[:, FC * SLOTS:, :].rearrange("p c d -> p (c d)")[:, u * 2 * ROW:(u + 1) * 2 * ROW].rearrange("p (c d) -> p c d", d=ROW)
            for u in range(SLOTS - TILES)]
        w2_raw = [x_raw[:, FC * u:FC * u + FC, :] for u in range(SLOTS)]
        ya = x_raw
        yb = xT_raw[:, 0:N].rearrange("p (t d) -> p t d", d=D)
        def diagonal(g, half):
            cs = g[:, half * CH // 2:(half + 1) * CH // 2, :, :, :].rearrange("p c a b d -> p c (a b) d")
            return cs[:, :, 0:4:3, :]

        psA = pb("psA", [P, 2, 1024])
        psG = pb("psG", [P, 2, 512])
        psO = pb("psO", [P, 512])
        psS = pb("psS", [P, 512])
        psA_m = psA[:, 1, :].rearrange("p (h c d) -> p h c d", h=2, d=D)
        psA_k = psA[0:H, 0, :]
        psG_k = psG[:, 1, 0:2 * CH].rearrange("p (c n) -> p c n", n=2)
        psS_l = psS[:, 0:TILES * E].rearrange("p (t e) -> p t e", e=E)
        psO_z = psO[:, :].rearrange("p (t d) -> p t d", d=D)
        psO_c = psO[:, 0:(TILES + 1) * E].rearrange("p (t e) -> p t e", e=E)
        psX = [psG[:, v, 0:BLK] for v in range(2)]
        psH = [psA[:, v, :].rearrange("p (c s) -> p c s", c=FC) for v in range(2)]
        psY = [ps[:, 0:2 * D].rearrange("p (t d) -> p t d", d=D) for ps in (psO, psS)]

        in_c, in_fold, in_x0, in_x, in_small, in_bias = (sem(n) for n in ("in_c", "in_fold", "in_x0", "in_x", "in_small", "in_bias"))
        cleared, zero_ready, filled, b2_stored, bf_in = (sem(n) for n in ("cleared", "zero_ready", "filled", "b2_stored", "bf_in"))
        cast, bias_step, fold_pe, fold_hi, fold_lo, mean_pe, gwc_ready = (
            sem(n) for n in ("cast", "bias_step", "fold_pe", "fold_hi", "fold_lo", "mean_pe", "gwc_ready"))
        xT_h, xT_l, x_h, x_l = (sem(n) for n in ("xT_h", "xT_l", "x_h", "x_l"))
        k_pe, k_h, k_l, q_pe, q_done, g_pe, g_h, g_l, m_pe, m_h, m_l = (
            sem(n) for n in ("k_pe", "k_h", "k_l", "q_pe", "q_done", "g_pe", "g_h", "g_l", "m_pe", "m_h", "m_l"))
        ks_pe, krow_done, ksT_pe, ks_done, n_pe, n_step, bc_pe, qn_done, qn_h, qn_l, o_pe, zT_done = (
            sem(n) for n in ("ks_pe", "krow_done", "ksT_pe", "ks_done", "n_pe", "n_step", "bc_pe", "qn_done", "qn_h", "qn_l", "o_pe", "zT_done"))
        z_pe, l_pe, c_pe, st_step, ln_step, x1_done, route, exp_done, scattered, table = (
            sem(n) for n in ("z_pe", "l_pe", "c_pe", "st_step", "ln_step", "x1_done", "route", "exp_done", "scattered", "table"))
        e_x, e_w, e_v, e_out = ([sem(f"{n}{u}") for u in range(SLOTS)] for n in ("e_x", "e_w", "e_v", "e_out"))
        e_T, e_Th, e_Tl, e_wh, e_wl, e_up, e_gelu, e_down, e_y0, e_y = (
            sem(n) for n in ("e_T", "e_Th", "e_Tl", "e_wh", "e_wl", "e_up", "e_gelu", "e_down", "e_y0", "e_y"))
        in_sel, g_cleared, tab_step, qn_lp = sem("in_sel"), sem("g_cleared"), sem("tab_step"), sem("qn_lp")
        f_in, f_sum, f_out = ([sem(f"{n}{u}") for u in range(4)] for n in ("f_in", "f_sum", "f_out"))
        f_z, f_stats, f_ln, f_norm = (sem(n) for n in ("f_z", "f_stats", "f_ln", "f_norm"))

        N_STEPS, LN_STEPS, ST_STEPS, ROUTE_STEPS = 7, 15, 2 * TILES, 24
        TOP_AT, HOT_AT = 10, 13

        class Steps:

            def __init__(self, eng, which, done):
                self.eng, self.which, self.n = eng, which, done

            def __call__(self, ins):
                ins.then_inc(self.which, 1)
                self.n = self.n + 1

            def wait(self):
                self.eng.wait_ge(self.which, self.n)

        def wait_alone(eng, which, value):
            eng.wait_ge(which, value)
            eng.nop(nofuse=True)

        def batches(eng, body):
            body(0, False, True)
            body(1, True, True)
            with eng.Fori(2, B) as b:
                body(b, True, True)
            body(B, True, False)

        def blocks(eng, body):
            for u in range(SLOTS):
                body(u, u, 0)
            with eng.Fori(1, NBLK // SLOTS) as i:
                for u in range(SLOTS):
                    body(SLOTS * i + u, u, i)
            for u in range(NBLK % SLOTS):
                body(NBLK // SLOTS * SLOTS + u, u, NBLK // SLOTS)

        def earlier(n, u, i, back):
            return n - back, (u - back) % SLOTS, i - (u < back)

        last_blocks = [(n, n % SLOTS, n // SLOTS) for n in (NBLK - 2, NBLK - 1)]

        def later(n, least):
            return not isinstance(n, int) or n >= least

        def groups(body):
            for h in range(2):
                for j in range(4):
                    body(h, j, 4 * h + j)

        block = ctx.enter_context(nc.Block())

        @block.sync
        def _(sp):
            sp.wait_ge(cleared, 2)
            sp.dma_start(wqkvT_sb, wqkvT.rearrange("(c p) d -> p c d", p=P)).then_inc(in_fold, 16)
            for r in (0, DH):
                sp.dma_start(wfd[r:r + DH, r:r + DH], wf).then_inc(in_fold, 16)
            wout_v = wout.rearrange("(c a p) n -> a p c n", a=2, p=DH)
            for a in range(2):
                sp.dma_start(woutd[DH * a:DH * a + DH, :, a, :], wout_v[a]).then_inc(in_fold, 16)
            x_v = x.rearrange("(t p) d -> p t d", p=P)
            sp.dma_start(xT_raw[:, 0:S], xT[:, 0:S]).then_inc(in_x0, 16)
            sp.dma_start(x_raw[:, 0:TILES, :], x_v[:, 0:TILES, :]).then_inc(in_x0, 16)
            sp.dma_start(xT_raw[:, S:N], xT[:, S:]).then_inc(in_x, 16)
            sp.dma_start(x_raw[:, TILES:, :], x_v[:, TILES:, :]).then_inc(in_x, 16)
            sp.wait_ge(zero_ready, 2)
            sp.wait_ge(bf_in, 48)
            sp.dma_start(xs.rearrange("(p r f) c -> p r (f c)", p=P, f=FILL),
                         zeros[:, :, :].rearrange("p f c -> p (f c)")[:, None, :]
                         .broadcast_to([P, XS_ROWS // P // FILL, FILL * ROW])).then_inc(filled, 16)

            sp.wait_ge(b2_stored, 48)
            sp.wait_ge(table, 2)

            def load_weights(n, u):
                expert = sp.value_load(tabi[0:1, 0, ds(n, 1)], min_val=0, max_val=E - 1)
                sp.dma_start(w1_raw[u], w1[ds(expert, 1), :, :].rearrange("a p n -> (a p) n")).then_inc(e_w[u], 16)
                sp.dma_start(w2_raw[u][:, :, :], w2[ds(expert, 1), :, :].rearrange("a p (c n) -> (a p) c n", c=FC)).then_inc(e_v[u], 16)
                sp.dma_start(b2_row[u][:, :], b2p[:, ds(expert * D + S, D)]).then_inc(e_v[u], 16)

            def load_rows(n, u):
                first = sp.value_load(tabi[0:1, 1, ds(n, 1)], min_val=0, max_val=NOWHERE)
                sp.dma_start(xrow[u], xs[ds(first, BLK), :].rearrange("(c p) d -> p c d", p=P)).then_inc(e_x[u], 16)

            for u in range(SLOTS):
                load_weights(u, u)
            sp.wait_ge(scattered, 16 * TILES * TOPK * B)
            for u in range(SLOTS):
                load_rows(u, u)

            def load(n, u, i):
                if isinstance(n, int) and n < SLOTS:
                    return
                wait_alone(sp, e_down, n - SLOTS + 1)
                load_weights(n, u)
                wait_alone(sp, e_y, n - SLOTS + 1)
                wait_alone(sp, e_out[u], 32 * i)
                load_rows(n, u)
            blocks(sp, load)

            for u in range(SLOTS):
                sp.wait_ge(e_out[u], 32 * ((NBLK - u + SLOTS - 1) // SLOTS))
            ya_v = ys[0:N, :].rearrange("(t p) d -> p t d", p=P)
            yb_v = ys[N:2 * N, :].rearrange("(t p) d -> p t d", p=P)

            def fetch(h, j, g):
                at = slice(g * TILES, (g + 1) * TILES)
                if h:
                    sp.wait_ge(f_sum[j], h)
                sp.dma_start(ya[:, at, :], ya_v[:, at, :]).then_inc(f_in[j], 16)
                sp.dma_start(yb[:, at, :], yb_v[:, at, :]).then_inc(f_in[j], 16)
            groups(fetch)

        @block.gpsimd
        def _(pool):
            pool.memset(wfd[:, :], 0.0).then_inc(cleared, 1)
            pool.memset(x1[:, 0:2 * CH, :], 0.0).then_inc(cleared, 1)
            pool.memset(xT_raw[:, N:], 0.0)
            for g in (g_hi, g_lo):
                pool.memset(g[:, :, :, :, :].rearrange("p c a b d -> p (c a b d)").bitcast(F32), 0.0).then_inc(g_cleared, 1)

            def low(out_, full_, hi_):
                return pool.tensor_tensor(out_, full_, hi_.bitcast(F32), ALU.subtract)

            def scatter(b, prev, cur):
                if prev:
                    for c in range(1, CH, 2):
                        pool.wait_ge(qn_h, CH * (b - 1) + c + 1)
                        low(qn_lo[:, c % 2, :], qn[:, c % 4, :], qn_hi[:, c % 2, :]).then_inc(qn_lp, 1)
                if cur:
                    pool.wait_ge(x_h, b + 1)
                    low(x_lo[:, :, :], x_raw[:, ds(b * TILES, TILES), :], x_hi[:, :, :]).then_inc(x_l, 1)
                    pool.wait_ge(xT_h, b + 2)
                    low(xT_lo[:, :], xT_raw[:, ds((b + 1) * S, S)], xT_hi[:, :]).then_inc(xT_l, 1)
                if not prev:
                    return
                if isinstance(b, int) and b == 1:
                    pool.wait_ge(filled, 16)
                wait_alone(pool, route, ROUTE_STEPS * b)
                for j in range(TILES):
                    for k in range(TOPK):
                        pool.indirect_dma_start(xs, bass.IndirectOffsetOnAxis(ap=pos[:, j, k:k + 1], axis=0),
                                                rows[:, j, k, :], None).then_inc(scattered, 16)
            pool.wait_ge(xT_h, 1)
            low(xT_lo[:, :], xT_raw[:, 0:S], xT_hi[:, :]).then_inc(xT_l, 1)
            batches(pool, scatter)

            def store(n, u, i):
                wait_alone(pool, e_y, n + 1)
                for c in range(2):
                    pool.indirect_dma_start(ys, bass.IndirectOffsetOnAxis(ap=xrow[u][:, c, D:D + 1].bitcast(I32), axis=0),
                                            yrow[u][:, c, :], None, bounds_check=TOPK * N - 1, oob_is_err=False).then_inc(e_out[u], 16)
            blocks(pool, store)

            def add(h, j, g):
                at = slice(g * TILES, (g + 1) * TILES)
                pool.wait_ge(f_in[j], 32 * (h + 1))
                pool.tensor_tensor(ya[:, at, :], ya[:, at, :], yb[:, at, :], ALU.add).then_inc(f_sum[j], 1)
            groups(add)

        @block.tensor
        def _(pe):
            mm = pe.matmul

            def three(outp, a_hi, a_lo, b_hi, b_lo, start=True, stop=True):
                mm(outp, a_hi, b_hi, start=start, stop=False)
                mm(outp, a_hi, b_lo, start=False, stop=False)
                return mm(outp, a_lo, b_hi, start=False, stop=stop)

            pe.wait_ge(in_fold, 80)
            for part in range(2):
                for c in range(CH):
                    last = mm(psA[:, part, c * P:(c + 1) * P], wqkvT_sb[:, part * CH + c, :], wfd[:, :], start=True, stop=True)
                last.then_inc(fold_pe, 1)
            for half in range(2):
                pe.wait_ge(fold_lo, half + 1)
                for c in range(CH // 2):
                    cc = half * CH // 2 + c
                    last = mm(psA[:, half, c * 256:(c + 1) * 256], wqkvT_sb[:, 2 * CH + cc, :], woutd[:, cc, :, :], start=True, stop=True)
                last.then_inc(fold_pe, 1)
            pe.wait_ge(in_c, 16)
            pe.wait_ge(in_small, 64)
            mm(psS[:, 0:E], con("ones"), gw[:, :], start=True, stop=True).then_inc(mean_pe, 1)
            pe.wait_ge(cast, 8)
            pe.wait_ge(bf_in, 48)
            pe.wait_ge(gwc_ready, 1)
            pe.wait_ge(fold_lo, 4)

            def attention(b, prev, cur):
                def spread(c):
                    if c == 0:
                        pe.wait_ge(n_step, N_STEPS * b)
                        pe.wait_ge(g_l, 2 * b)
                    if c >= 2:
                        pe.wait_ge(qn_done, CH * (b - 1) + c - 1)
                    mm(psG[:, c % 2, :], sel_b[:, c, :], rT[:, :], start=True, stop=True).then_inc(bc_pe, 1)

                def output(c):
                    if c == 0:
                        pe.wait_ge(m_l, 2 * b)
                        pe.wait_ge(route, ROUTE_STEPS * (b - 1))
                    pe.wait_ge(qn_lp if c % 2 else qn_l, CH // 2 * (b - 1) + c // 2 + 1)
                    three(psO[:, :], m_hi[:, c, :], m_lo[:, c, :], qn_hi[:, c % 2, :], qn_lo[:, c % 2, :],
                          start=c == 0, stop=c == CH - 1).then_inc(o_pe, 1)

                def keys(t):
                    if t == 0:
                        pe.wait_ge(xT_l, b + 1)
                    if t == 1 and prev:
                        pe.wait_ge(m_l, 2 * b)
                    if t >= 2:
                        pe.wait_ge(k_l, TILES * b + t - 1)
                    at = slice(t * P, (t + 1) * P)
                    for h in range(2):
                        to = psA[:, t % 2, h * 512:(h + 1) * 512]
                        cols = slice(h * 512, (h + 1) * 512)
                        mm(to, ones_b[0:3, :], bf_rows[:, :], start=True, stop=False)
                        mm(to, xT_hi[:, at], wk_hi[:, cols], start=False, stop=False)
                        mm(to, xT_hi[:, at], wk_lo[:, cols], start=False, stop=False)
                        last = mm(to, xT_lo[:, at], wk_hi[:, cols], start=False, stop=True)
                    last.then_inc(k_pe, 1)

                def queries(i):
                    if i < 2:
                        pe.wait_ge(k_l, TILES * b + i + 3)
                    elif i == 2:
                        pe.wait_ge(q_done, CH // 2 * b + 2)
                    else:
                        pe.wait_ge(krow_done, b + 1)
                    for j in range(2):
                        c = 2 * i + j
                        at = slice(c * P, (c + 1) * P)
                        last = three(psA[:, (i + i // 2) % 2, j * 512:(j + 1) * 512], wq_hi[:, at], wq_lo[:, at], xT_hi[:, :], xT_lo[:, :])
                    last.then_inc(q_pe, 1)

                def logits():
                    pe.wait_ge(zT_done, b)
                    for j in range(TILES):
                        last = mm(psS_l[:, j, :], zT[:, j * P:(j + 1) * P], gwc[:, :], start=True, stop=True)
                    last.then_inc(l_pe, 1)
                    for j in range(TILES):
                        last = pe.transpose(psO_z[:, j, :], zT[:, j * P:(j + 1) * P], con("ident"))
                    last.then_inc(z_pe, 1)

                def ranks():
                    pe.wait_ge(x1_done, TILES * b)
                    pe.wait_ge(route, ROUTE_STEPS * (b - 1) + HOT_AT)
                    mm(psO_c[:, :, :], tri_b[:, :], hot_sum[:, :, :], start=True, stop=False)
                    for j in range(TILES):
                        last = mm(psO_c[:, j + 1:, :], ones_b[:, :], hot_sum[:, j:j + 1, :].broadcast_to([P, TILES - j, E]),
                                  start=False, stop=j == TILES - 1)
                    last.then_inc(c_pe, 1)

                def sums():
                    pe.wait_ge(q_done, CH // 2 * b + 1)
                    pe.wait_ge(k_l, TILES * (b + 1))
                    for h in range(2):
                        cols = slice(h * 512, (h + 1) * 512)
                        for t in range(TILES):
                            mm(psA_k[:, cols], ones_r[:, :], k_hi[:, t, cols], start=t == 0, stop=False)
                            last = mm(psA_k[:, cols], ones_r[:, :], k_lo[:, t, cols], start=False, stop=t == TILES - 1)
                    last.then_inc(ks_pe, 1)

                def turn_sums():
                    pe.wait_ge(krow_done, b + 1)
                    if prev:
                        pe.wait_ge(qn_done, CH * b)
                    for c in range(CH):
                        last = mm(psG_k[:, c, :], krow[0:1, c * P:(c + 1) * P], con("ones", 1)[:, 0:2], start=True, stop=True)
                    last.then_inc(ksT_pe, 1)

                def gram(h):
                    if h == 0:
                        pe.wait_ge(x_l, b + 1)
                    else:
                        pe.wait_ge(ks_done, b + 1)
                    cols = slice(h * 512, (h + 1) * 512)
                    for t in range(TILES):
                        last = three(psG[:, h, :], x_hi[:, t, :], x_lo[:, t, :], k_hi[:, t, cols], k_lo[:, t, cols],
                                     start=t == 0, stop=t == TILES - 1)
                    last.then_inc(g_pe, 1)

                def norms():
                    pe.wait_ge(ks_done, b + 1)
                    pe.wait_ge(q_done, CH // 2 * b + 3)
                    if prev:
                        pe.wait_ge(route, ROUTE_STEPS * (b - 1) + 1)
                    for c in range(CH):
                        if c == 6:
                            pe.wait_ge(q_done, CH // 2 * (b + 1))
                        last = mm(psS[:, :], ksd[:, c, :, :].rearrange("p r h -> p (r h)"), q_act[:, c, :], start=c == 0, stop=c == CH - 1)
                    last.then_inc(n_pe, 1)

                def mix(half):
                    pe.wait_ge(g_l, 2 * b + half + 1)
                    for i in range(CH // 2):
                        c = half * CH // 2 + i
                        for a in range(2):
                            cols = slice((2 * c + a) * D, (2 * c + a + 1) * D)
                            g = [part[:, c, a, :, :].rearrange("p b d -> p (b d)") for part in (g_hi, g_lo)]
                            last = three(psA_m[:, half, i, :], *g, vo_hi[:, cols], vo_lo[:, cols], start=a == 0, stop=a == 1)
                    last.then_inc(m_pe, 1)

                if prev:
                    spread(0)
                    spread(1)
                if cur:
                    keys(0)
                if prev:
                    spread(2)
                if cur:
                    keys(1)
                for t in range(TILES):
                    if prev:
                        if 2 < 2 * t + 2 < CH:
                            spread(2 * t + 2)
                        output(2 * t)
                        if 2 * t + 3 < CH:
                            spread(2 * t + 3)
                        output(2 * t + 1)
                    if cur:
                        (keys if t < 2 else queries)((t + 2) % TILES)
                if prev:
                    logits()
                if cur:
                    sums()
                    queries(2)
                    turn_sums()
                    queries(3)
                    norms()
                if prev:
                    ranks()
                if cur:
                    gram(0)
                    gram(1)
                    mix(0)
                    mix(1)
            batches(pe, attention)

            def turn_rows(n, u, i):
                pe.wait_ge(e_x[u], 16 * i + 16)
                if later(n, 2):
                    pe.wait_ge(e_Tl, n - 1)
                for c in range(2):
                    last = pe.transpose(psX[u % 2][:, c * P:(c + 1) * P], xrow[u][:, c, 0:D], con("ident"))
                last.then_inc(e_T, 1)

            def first_layer(n, u, i):
                v = u % 2
                pe.wait_ge(e_Tl, n + 1)
                pe.wait_ge(e_wl, n + 1)
                if later(n, 2):
                    pe.wait_ge(e_gelu, FC * (n - 1))
                at = slice(v * BLK, (v + 1) * BLK)
                for c in range(FC):
                    w = slice(v * F + c * P, v * F + (c + 1) * P)
                    last = three(psH[v][:, c, :], wq_hi[:, w], wq_lo[:, w], xT_hi[:, at], xT_lo[:, at])
                    last.then_inc(e_up, 1)

            def second_layer(n, u, i):
                v = u % 2
                pe.wait_ge(e_v[u], 32 * i + 32)
                pe.wait_ge(e_gelu, FC * (n + 1))
                if later(n, 2):
                    pe.wait_ge(e_y, n - 1)
                for t in range(2):
                    mm(psY[v][:, t, :], ones_b[0:3, :], b2_row[u][:, :], start=True, stop=False)
                    for c in range(FC):
                        last = mm(psY[v][:, t, :], hT[v][:, c, t * P:(t + 1) * P], w2_raw[u][:, c, :], start=False, stop=c == FC - 1)
                last.then_inc(e_down, 1)

            def experts(n, u, i):
                turn_rows(n, u, i)
                if later(n, 1):
                    first_layer(*earlier(n, u, i, 1))
                if later(n, 2):
                    second_layer(*earlier(n, u, i, 2))
            blocks(pe, experts)
            first_layer(*last_blocks[1])
            second_layer(*last_blocks[0])
            second_layer(*last_blocks[1])

        @block.scalar
        def _(act):
            def hi(out_, in_, func=ACT.Copy, **kw):
                return act.activation(out_, in_, func, **kw)

            act.dma_start(cst[:, :], consts[:, 0:C_KEPT]).then_inc(in_c, 16)
            act.dma_start(sel_f, consts[:, C_KEPT:]).then_inc(in_sel, 16)
            act.dma_start(bias_raw[:, 0:S].rearrange("p (h d) -> p h d", d=DH), bf[None, None, :].broadcast_to([1, S // DH, DH])).then_inc(in_bias, 16)
            act.dma_start(bias_raw[:, S:], b2).then_inc(in_bias, 16)
            act.dma_start(gw[:, :], gwT).then_inc(in_small, 16)
            act.dma_start(bout_col[:, :], bout.rearrange("(d a) -> d a", a=1)).then_inc(in_small, 16)
            act.dma_start(bf_col[0:DH, :], bf.rearrange("(d a) -> d a", a=1)).then_inc(in_small, 16)
            act.dma_start(bf_col[DH:P, :], bf.rearrange("(d a) -> d a", a=1)).then_inc(in_small, 16)
            act.wait_ge(bias_step, 5)
            for i in range(3):
                act.dma_start(bf_rows[i:i + 1, :], bias_row[i][:, 0:S]).then_inc(bf_in, 16)
                act.dma_start(b2p[i:i + 1, :], bias_row[i]).then_inc(b2_stored, 16)
            folded = [(wq_hi[:, :], 0), (wk_hi[:, :], 1), (vo_hi[:, 0:1024], 0), (vo_hi[:, 1024:], 1)]
            for i, (to, half) in enumerate(folded):
                act.wait_ge(fold_pe, i + 1)
                hi(to, psA[:, half, :]).then_inc(fold_hi, 1)
            act.wait_ge(in_x0, 32)
            hi(xT_hi[:, :], xT_raw[:, 0:S]).then_inc(xT_h, 1)

            def attention(b, prev, cur):
                def out_hi(c):
                    act.wait_ge(qn_done, CH * (b - 1) + c + 1)
                    act.wait_ge(o_pe, CH * (b - 1) + max(c - 1, 0))
                    hi(qn_hi[:, c % 2, :], qn[:, c % 4, :]).then_inc(qn_h, 1)

                def key_hi(t):
                    act.wait_ge(k_pe, TILES * b + t + 1)
                    if t == 0:
                        act.wait_ge(g_pe, 2 * b)
                        act.wait_ge(ks_pe, b)
                    hi(k_hi[:, t, :], psA[:, t % 2, :], ACT.Relu).then_inc(k_h, 1)

                def query(i):
                    act.wait_ge(q_pe, CH // 2 * b + i + 1)
                    if prev:
                        act.wait_ge(n_pe, b)
                        act.wait_ge(qn_done, CH * (b - 1) + 2 * i + 2)
                    hi(q_act[:, 2 * i:2 * i + 2, :], psA[:, (i + i // 2) % 2, :].rearrange("p (c s) -> p c s", c=2), ACT.Relu,
                       bias=bf_col[:, 0:1]).then_inc(q_done, 1)

                if prev:
                    out_hi(0)
                if cur:
                    key_hi(0)
                for t in range(TILES):
                    if prev:
                        if t:
                            out_hi(2 * t)
                        out_hi(2 * t + 1)
                    if cur:
                        if t + 1 < TILES:
                            key_hi(t + 1)
                        else:
                            query(0)
                if cur:
                    query(1)
                    act.wait_ge(g_pe, 2 * b)
                    hi(x_hi[:, :, :], x_raw[:, ds(b * TILES, TILES), :]).then_inc(x_h, 1)
                    act.wait_ge(ks_pe, b + 1)
                    if prev:
                        act.wait_ge(o_pe, CH * b)
                    hi(krow[:, :], psA_k[0:1, :]).then_inc(krow_done, 1)
                    query(2)
                    query(3)
                if prev:
                    act.wait_ge(ln_step, LN_STEPS * b)
                    for j in range(TILES):
                        act.activation(x1[:, ds((b - 1) * TILES + j, 1), :], psO_z[:, j:j + 1, :], ACT.Identity,
                                       bias=ln[:, 3, j:j + 1], scale=ln[:, 1, j:j + 1]).then_inc(x1_done, 1)
                    act.wait_ge(route, ROUTE_STEPS * (b - 1) + TOP_AT)
                    act.activation(tope[:, :, :], topd[:, :, :], ACT.Exp).then_inc(exp_done, 1)
                if cur:
                    if isinstance(b, int) and b == 0:
                        act.wait_ge(in_x, 32)
                    act.wait_ge(q_pe, CH // 2 * (b + 1))
                    hi(xT_hi[:, :], xT_raw[:, ds((b + 1) * S, S)]).then_inc(xT_h, 1)
                    for h in range(2):
                        act.wait_ge(g_pe, 2 * b + h + 1)
                        if h == 0:
                            act.wait_ge(g_cleared, 2)
                            act.wait_ge(m_pe, 2 * b)
                        hi(diagonal(g_hi, h), psG[:, h, :].rearrange("p (c a d) -> p c a d", a=2, d=DH)).then_inc(g_h, 1)
                    for h in range(2):
                        act.wait_ge(m_pe, 2 * b + h + 1)
                        if h == 0:
                            act.wait_ge(o_pe, CH * b)
                        hi(m_hi[:, h * CH // 2:(h + 1) * CH // 2, :], psA_m[:, h, :, :]).then_inc(m_h, 1)
            batches(act, attention)
            act.wait_ge(xT_l, B + 1)

            def gelu(n, u, i):
                v = u % 2
                act.wait_ge(e_w[u], 16 * i + 16)
                for c in range(FC):
                    act.wait_ge(e_up, FC * n + c // 2 * 2 + 2)
                    if c == 0 and later(n, 2):
                        act.wait_ge(e_down, n - 1)
                    act.activation(hT[v][:, c, :], psH[v][:, c, :], ACT.Gelu_apprx_tanh,
                                   bias=w1_raw[u][:, F + c:F + c + 1]).then_inc(e_gelu, 1)

            def experts(n, u, i):
                act.wait_ge(e_T, n + 1)
                if later(n, 2):
                    act.wait_ge(e_up, FC * (n - 1))
                v = u % 2
                hi(xT_hi[:, v * BLK:(v + 1) * BLK], psX[v]).then_inc(e_Th, 1)
                if later(n, 1):
                    gelu(*earlier(n, u, i, 1))
            blocks(act, experts)
            gelu(*last_blocks[1])

            out_v = out.rearrange("b (t p) d -> p (b t) d", p=P)

            def finish(h, j, g):
                act.wait_ge(f_ln, LN_STEPS * (h + 1))
                for t in range(TILES):
                    at = slice(g * TILES + t, g * TILES + t + 1)
                    col = slice(j * TILES + t, j * TILES + t + 1)
                    act.activation(yb[:, at, :], x1[:, at, :], ACT.Identity,
                                   bias=ln[:, 3, col], scale=ln[:, 1, col]).then_inc(f_norm, 1)
                act.wait_ge(f_norm, TILES * (g + 1))
                at = slice(g * TILES, (g + 1) * TILES)
                act.dma_start(out_v[:, at, :], yb[:, at, :]).then_inc(f_out[j], 16)
            groups(finish)
            for j in range(4):
                act.wait_ge(f_out[j], 32)

        @block.vector
        def _(dve):
            def lo(out_, full_, hi_):
                return dve.tensor_tensor(out_, full_, hi_.bitcast(F32), ALU.subtract)

            def norm_steps(step, cols):
                v, y, t, nb = (ln[:, i, cols] for i in range(4))
                step(dve.tensor_scalar(v, mv[:, cols, 1], LN_EPS, None, ALU.add))
                step.wait()
                step(dve.tensor_scalar(y.bitcast(I32), v.bitcast(I32), -0.5, RSQRT_SEED, ALU.mult, ALU.add))
                for _ in range(3):
                    step.wait()
                    step(dve.tensor_tensor(t, v, y, ALU.mult))
                    step.wait()
                    step(dve.tensor_tensor(t, t, y, ALU.mult))
                    step.wait()
                    step(dve.tensor_scalar(t, t, -0.5, 1.5, ALU.mult, ALU.add))
                    step.wait()
                    step(dve.tensor_tensor(y, y, t, ALU.mult))
                step.wait()
                step(dve.scalar_tensor_tensor(nb, mv[:, cols, 0], -1.0, y, ALU.mult, ALU.mult))

            dve.memset(zeros[:, :, :], 0.0).then_inc(zero_ready, 1)
            dve.wait_ge(zero_ready, 1)
            dve.memset(zeros[:, :, D:D + 1].bitcast(I32), 65535).then_inc(zero_ready, 1)
            dve.memset(rows[:, :, :, :], 0.0).then_inc(cast, 1)
            dve.memset(hot_sum[:, :, :], 0.0).then_inc(cast, 1)
            dve.wait_ge(in_c, 16)
            dve.tensor_copy(ones_r[:, :], con("ones")[:, 0:H]).then_inc(cast, 1)
            dve.tensor_copy(ones_b[:, :], con("ones")).then_inc(cast, 1)
            dve.tensor_copy(tri_b[:, :], con("tri")).then_inc(cast, 1)
            dve.wait_ge(in_sel, 16)
            dve.tensor_copy(sel_b[:, :, :], sel_f.rearrange("p (c m) -> p c m", c=CH)).then_inc(cast, 1)
            dve.tensor_copy(base[:, :], con("first")).then_inc(cast, 1)
            dve.tensor_copy(dest[:, :, :], con("dest").rearrange("p (t k) -> p t k", k=TOPK)).then_inc(cast, 1)
            dve.wait_ge(in_bias, 32)
            step = Steps(dve, bias_step, 0)
            for i in range(3):
                step(dve.tensor_copy(bias_row[i], bias_raw[:, :]))
                step.wait()
                if i < 2:
                    step(dve.tensor_tensor(bias_raw[:, :], bias_raw[:, :], bias_row[i], ALU.subtract))
                    step.wait()
            folded = [(wq_hi[:, :], wq_lo[:, :], 0), (wk_hi[:, :], wk_lo[:, :], 1),
                      (vo_hi[:, 0:1024], vo_lo[:, 0:1024], 0), (vo_hi[:, 1024:], vo_lo[:, 1024:], 1)]
            for i, (h_, l_, half) in enumerate(folded):
                dve.wait_ge(fold_hi, i + 1)
                lo(l_, psA[:, half, :], h_).then_inc(fold_lo, 1)
            dve.wait_ge(b2_stored, 48)
            dve.wait_ge(bf_in, 48)
            dve.wait_ge(mean_pe, 1)
            dve.wait_ge(in_small, 64)
            dve.scalar_tensor_tensor(gwc[:, :], psS[:, 0:E], -1.0 / D, gw[:, :], ALU.mult, ALU.add).then_inc(gwc_ready, 1)

            def attention(b, prev, cur):
                def normalise(c):
                    dve.wait_ge(bc_pe, CH * (b - 1) + c + 1)
                    if c >= 4 and c % 2:
                        dve.wait_ge(qn_lp, CH // 2 * (b - 1) + c // 2 - 1)
                    elif c >= 4:
                        dve.wait_ge(qn_l, CH // 2 * (b - 1) + c // 2 - 1)
                    dve.tensor_tensor(qn[:, c % 4, :], q_act[:, c, :], psG[:, c % 2, :], ALU.mult).then_inc(qn_done, 1)

                def out_lo(c):
                    dve.wait_ge(qn_h, CH * (b - 1) + c + 1)
                    lo(qn_lo[:, c % 2, :], qn[:, c % 4, :], qn_hi[:, c % 2, :]).then_inc(qn_l, 1)

                def key_lo(t):
                    dve.wait_ge(k_h, TILES * b + t + 1)
                    dve.scalar_tensor_tensor(k_lo[:, t, :], psA[:, t % 2, :], 0.0, k_hi[:, t, :].bitcast(F32),
                                             ALU.max, ALU.subtract).then_inc(k_l, 1)

                step = Steps(dve, route, ROUTE_STEPS * (b - 1))

                def choose():
                    wait_alone(dve, step.which, step.n)
                    for j in range(TILES):
                        step(dve.max(top[:, j, :], logit[:, j, :]))
                    wait_alone(dve, step.which, step.n)
                    for j in range(TILES):
                        step(dve.max_index(topi[:, j, :], top[:, j, :], logit[:, j, :]))
                    step(dve.tensor_tensor(topd[:, :, :], top[:, :, :], top[:, :, 0:1].broadcast_to([P, TILES, 8]), ALU.subtract))
                    step.wait()
                    step(dve.tensor_copy(topf[:, :, :], topi[:, :, 0:TOPK]))
                    step.wait()
                    step(dve.tensor_tensor(hot[:, :, :, :].rearrange("p t k e -> p (t k) e"),
                                           con("iota")[:, None, :].broadcast_to([P, TILES * TOPK, E]),
                                           topf[:, :, :].rearrange("p t k -> p (t k)")[:, :, None].broadcast_to([P, TILES * TOPK, E]),
                                           ALU.is_equal))
                    step.wait()
                    step(dve.tensor_tensor(hot_sum[:, 0:TILES, :], hot[:, :, 0, :], hot[:, :, 1, :], ALU.add))
                    dve.wait_ge(exp_done, b)
                    step(dve.tensor_reduce(den[:, 0, :], tope[:, :, :], AX_X, ALU.add))
                    step.wait()
                    step(dve.reciprocal(den[:, 1, :], den[:, 0, :]))
                    step.wait()
                    dve.wait_ge(scattered, 16 * TILES * TOPK * (b - 1))
                    step(dve.tensor_tensor(rows[:, :, :, D + 1], tope[:, :, 0:TOPK],
                                           den[:, 1, :][:, :, None].broadcast_to([P, TILES, TOPK]), ALU.mult))
                    step(dve.tensor_copy(rows[:, :, :, D].bitcast(I32), dest[:, :, :]))
                    step.wait()
                    step(dve.tensor_scalar(dest[:, :, :], dest[:, :, :], float(S), None, ALU.add))
                    dve.wait_ge(x1_done, TILES * b)
                    step(dve.tensor_copy(rows[:, :, :, 0:D],
                                         x1[:, ds((b - 1) * TILES, TILES), :][:, :, None, :].broadcast_to([P, TILES, TOPK, D])))

                def place():
                    dve.wait_ge(c_pe, b)
                    step(dve.tensor_tensor(rank[:, :, :], psO_c[:, 0:TILES, :], base[:, None, :].broadcast_to([P, TILES, E]), ALU.add))
                    step.wait()
                    step(dve.tensor_tensor(base[:, :], base[:, :], psO_c[:, TILES, :], ALU.add))
                    step(dve.tensor_tensor(picked[:, :, :, :], hot[:, :, :, :],
                                           rank[:, :, None, :].broadcast_to([P, TILES, TOPK, E]), ALU.mult))
                    step.wait()
                    step(dve.tensor_reduce(posf[:, :, :], picked[:, :, :, :], AX_X, ALU.add))
                    step.wait()
                    step(dve.tensor_copy(pos[:, :, :], posf[:, :, :]))

                if prev:
                    normalise(0)
                    normalise(1)
                if cur and not prev:
                    key_lo(0)
                for t in range(TILES):
                    if prev:
                        out_lo(2 * t)
                        if t < TILES - 1:
                            normalise(2 * t + 2)
                        if cur and t == 0:
                            key_lo(0)
                        if t < TILES - 1:
                            normalise(2 * t + 3)
                    if cur and t + 1 < TILES:
                        key_lo(t + 1)
                if prev:
                    dve.wait_ge(o_pe, CH * b)
                    dve.scalar_tensor_tensor(zT[:, :], psO[:, :], bout_col[:, 0:1], xT_raw[:, ds((b - 1) * S, S)],
                                             ALU.add, ALU.add).then_inc(zT_done, 1)
                    dve.wait_ge(z_pe, b)
                    st = Steps(dve, st_step, ST_STEPS * (b - 1))
                    for j in range(TILES):
                        st(dve.bn_stats(stats[:, j, :], psO_z[:, j, :]))
                    wait_alone(dve, st.which, st.n)
                    for j in range(TILES):
                        st(dve.bn_aggr(mv[:, j, :], stats[:, j, :]))
                    st.wait()
                if prev:
                    norm_steps(Steps(dve, ln_step, LN_STEPS * (b - 1)), slice(0, TILES))
                    dve.wait_ge(ln_step, LN_STEPS * b)
                    dve.wait_ge(l_pe, b)
                    step(dve.tensor_tensor(logit[:, :, :], psS_l, ln[:, 1, 0:TILES][:, :, None].broadcast_to([P, TILES, E]), ALU.mult))
                if cur:
                    dve.wait_ge(ksT_pe, b + 1)
                    dve.wait_ge(n_pe, b)
                    dve.tensor_tensor(ksd[:, :, :, :], con("mask").rearrange("p (c h) -> p c h", h=H)[:, :, None, :].broadcast_to([P, CH, P // H, H]),
                                      psG_k[:, :, 0:1][:, :, :, None].broadcast_to([P, CH, P // H, H]), ALU.mult).then_inc(ks_done, 1)
                if prev:
                    choose()

                def gram_lo(h):
                    dve.wait_ge(g_h, 2 * b + h + 1)
                    lo(diagonal(g_lo, h), psG[:, h, :].rearrange("p (c a d) -> p c a d", a=2, d=DH), diagonal(g_hi, h)).then_inc(g_l, 1)

                def mixed_lo(h):
                    cs = slice(h * CH // 2, (h + 1) * CH // 2)
                    dve.wait_ge(m_h, 2 * b + h + 1)
                    lo(m_lo[:, cs, :], psA_m[:, h, :, :], m_hi[:, cs, :]).then_inc(m_l, 1)

                if cur:
                    dve.wait_ge(n_pe, b + 1)
                    ns = Steps(dve, n_step, N_STEPS * b)
                    ns(dve.tensor_scalar(rn[:, 0, :], psS[:, :], NORM_EPS, None, ALU.add))
                if prev:
                    place()
                if cur:
                    ns.wait()
                    for h in range(2):
                        half = slice(h * S // 2, (h + 1) * S // 2)
                        ns(dve.reciprocal(rn[:, 1, half], rn[:, 0, half]))
                        if h == 0:
                            gram_lo(0)
                    gram_lo(1)
                    ns.wait()
                    r1, r2 = slice(PARTS_AT[1] * H, P), slice(PARTS_AT[2] * H, P)
                    ns(dve.tensor_copy(rT[:, :], rn[:, 1, :]))
                    ns.wait()
                    ns(dve.tensor_tensor(rn[r1, 0, :], rn[r1, 1, :], rT[r1, :], ALU.subtract))
                    ns.wait()
                    ns(dve.tensor_copy(rT[r1, :], rn[r1, 0, :]))
                    ns.wait()
                    ns(dve.tensor_tensor(rT[r2, :], rn[r2, 0, :], rT[r2, :], ALU.subtract))
                    mixed_lo(0)
                    mixed_lo(1)
            batches(dve, attention)

            first_ = con("first", 1)
            dve.wait_ge(route, ROUTE_STEPS * B)
            tb = Steps(dve, tab_step, 0)
            tb(dve.tensor_tensor(cnt[:, 0, :], base[0:1, :], first_, ALU.subtract))
            tb.wait()
            tb(dve.tensor_tensor(full[:, :, :], cnt[:, 0, :][:, :, None].broadcast_to([1, E, 16]),
                                 con("step", 1).rearrange("p (e s) -> p e s", e=E), ALU.is_gt))
            tb.wait()
            tb(dve.tensor_reduce(cnt[:, 1, :], full[:, :, :], AX_X, ALU.add))
            tb.wait()
            tb(dve.tensor_tensor(upto_n[:, :, :], con("upto", 1).rearrange("p (a e) -> p a e", a=E),
                                 cnt[:, 1:2, :].broadcast_to([1, E, E]), ALU.mult))
            tb.wait()
            tb(dve.tensor_reduce(cnt[:, 2, :], upto_n[:, :, :], AX_X, ALU.add))
            tb.wait()
            tb(dve.tensor_tensor(past[:, 0, :, :], cnt[:, 2:3, :].broadcast_to([1, NBLK, E]),
                                 con("block", 1)[:, :, None].broadcast_to([1, NBLK, E]), ALU.is_le))
            tb.wait()
            tb(dve.tensor_reduce(tab[:, 0, :], past[:, 0, :, :], AX_X, ALU.add))
            tb(dve.tensor_tensor(past[:, 1, :, :], past[:, 0, :, :], cnt[:, 1:2, :].broadcast_to([1, NBLK, E]), ALU.mult))
            tb.wait()
            tb(dve.tensor_reduce(tab[:, 1, :], past[:, 1, :, :], AX_X, ALU.add))
            tb.wait()
            tb(dve.tensor_tensor(tab[:, 2, :], con("block", 1), tab[:, 1, :], ALU.subtract))
            tb.wait()
            tb(dve.tensor_scalar(tab[:, 3, :], tab[:, 2, :], float(BLK), None, ALU.mult))
            tb.wait()
            tb(dve.scalar_tensor_tensor(tab[:, 4, :], tab[:, 0, :], float(REGION), tab[:, 3, :], ALU.mult, ALU.add))
            tb.wait()
            dve.tensor_scalar(tabi[:, 0, :], tab[:, 0, :], float(E - 1), None, ALU.min).then_inc(table, 1)
            dve.tensor_scalar(tabi[:, 1, :], tab[:, 4, :], float(NOWHERE), None, ALU.min).then_inc(table, 1)

            def result(n, u, i):
                v = u % 2
                dve.wait_ge(e_down, n + 1)
                if later(n, SLOTS):
                    dve.wait_ge(e_out[u], 32 * i)
                dve.tensor_scalar(yrow[u][:, 0, :], psY[v][:, 0, :], xrow[u][:, 0, D + 1:D + 2], None, ALU.mult).then_inc(e_y0, 1)
                dve.tensor_scalar(yrow[u][:, 1, :], psY[v][:, 1, :], xrow[u][:, 1, D + 1:D + 2], None, ALU.mult).then_inc(e_y, 1)

            def experts(n, u, i):
                v = u % 2
                at, ws = slice(v * BLK, (v + 1) * BLK), slice(v * F, (v + 1) * F)
                dve.wait_ge(e_w[u], 16 * i + 16)
                if later(n, 2):
                    dve.wait_ge(e_up, FC * (n - 1))
                dve.tensor_copy(wq_hi[:, ws], w1_raw[u][:, 0:F]).then_inc(e_wh, 1)
                dve.wait_ge(e_wh, n + 1)
                lo(wq_lo[:, ws], w1_raw[u][:, 0:F], wq_hi[:, ws]).then_inc(e_wl, 1)
                dve.wait_ge(e_Th, n + 1)
                lo(xT_lo[:, at], psX[v], xT_hi[:, at]).then_inc(e_Tl, 1)
                if later(n, 2):
                    result(*earlier(n, u, i, 2))
            blocks(dve, experts)
            result(*last_blocks[0])
            result(*last_blocks[1])


            def add_and_measure(h, j, g):
                at = slice(g * TILES, (g + 1) * TILES)
                dve.wait_ge(f_sum[j], h + 1)
                dve.tensor_tensor(x1[:, at, :], x1[:, at, :], ya[:, at, :], ALU.add).then_inc(f_z, 1)
                wait_alone(dve, f_z, g + 1)
                st = Steps(dve, f_stats, ST_STEPS * g)
                for t in range(TILES):
                    st(dve.bn_stats(stats[:, j * TILES + t, :], x1[:, g * TILES + t, :]))
                wait_alone(dve, st.which, st.n)
                if h and j == 0:
                    wait_alone(dve, f_ln, LN_STEPS)
                for t in range(TILES):
                    st(dve.bn_aggr(mv[:, j * TILES + t, :], stats[:, j * TILES + t, :]))
                if j == 3:
                    st.wait()
                    if h:
                        dve.wait_ge(f_norm, 4 * TILES)
                    norm_steps(Steps(dve, f_ln, LN_STEPS * h), slice(0, 4 * TILES))
            groups(add_and_measure)


def kernel(L0_attn_x, L0_attn_W_qkv, L0_attn_W_f, L0_attn_b_f, L0_attn_W_out, L0_attn_b_out,
           L0_ffn_gate_w, L0_ffn_w1, L0_ffn_b1, L0_ffn_w2, L0_ffn_b2):
    import concourse.bacc as bacc
    from concourse.bass_utils import run_bass_kernel_spmd

    def f(a):
        return np.ascontiguousarray(a)
    x = np.asarray(L0_attn_x).reshape(N, D)
    w1 = np.transpose(np.asarray(L0_ffn_w1), (1, 2, 0))
    b1 = np.transpose(np.asarray(L0_ffn_b1).reshape(E, FC, P), (0, 2, 1))
    w2 = np.transpose(np.asarray(L0_ffn_w2).reshape(D, E, FC, P), (1, 3, 2, 0)).reshape(E, P, FC * D)
    arrays = {
        "x": f(x), "xT": f(x.T), "wqkvT": f(np.asarray(L0_attn_W_qkv).T), "wf": f(L0_attn_W_f), "bf": f(L0_attn_b_f),
        "wout": f(L0_attn_W_out), "bout": f(L0_attn_b_out), "gwT": f(np.asarray(L0_ffn_gate_w).T),
        "w1": f(np.concatenate([w1, b1], axis=2)), "w2": f(w2), "b2": f(np.asarray(L0_ffn_b2).reshape(1, E * D)),
        "consts": shape_constants(),
    }
    nc = bacc.Bacc("TRN2", target_bir_lowering=False, num_devices=1)
    args = {n: nc.dram_tensor(n, a.shape, mybir.dt.from_np(a.dtype), kind="ExternalInput").ap() for n, a in arrays.items()}
    out = nc.dram_tensor("out", (B, S, D), F32, kind="ExternalOutput").ap()
    program(nc, out=out, **args)
    r = run_bass_kernel_spmd(nc, [arrays], core_ids=[0])
    return r.results[0]["out"]
```

```python
from contextlib import ExitStack

import numpy as np

import concourse.bass as bass
from concourse import mybir

ALU = mybir.AluOpType
ACT = mybir.ActivationFunctionType
AX_X = mybir.AxisListType.X
F32 = mybir.dt.float32
F32R = mybir.dt.float32r
BF16 = mybir.dt.bfloat16
I32 = mybir.dt.int32
U32 = mybir.dt.uint32
ds = bass.ds

P = 128
D = 128
B, S = 8, 512
N = B * S
TILES = S // P
H, DH = 16, 64
HD = H * DH
CH = HD // P
E, F = 8, 512
FC = F // P
TOPK = 2
BLK = 256
NBLK = (N * TOPK + E * (BLK - 1)) // BLK
REGION = N + BLK
ROW = D + 4
XS_ROWS = E * REGION + BLK
NOWHERE = E * REGION
LN_EPS = 1e-5
NORM_EPS = 1e-6
RSQRT_SEED = float(0x5F3759DF)
R_RING = 4
SLOTS = 6
W_ROW = F + FC + FC * D + D

_C = {}
_at = 0
for _name, _n in (("ident", P), ("tri", P), ("ones", P), ("mask", CH * H), ("iota", E), ("dest", TILES * TOPK),
                  ("first", E), ("block", NBLK), ("step", E * 16), ("upto", E * E)):
    _C[_name] = (_at, _at + _n)
    _at += _n
C_COLS = _at


def shape_constants():
    c = np.zeros((P, C_COLS), np.float32)

    def put(name, value):
        lo, hi = _C[name]
        value = np.asarray(value, np.float32).reshape(-1, hi - lo)
        c[:len(value) if len(value) > 1 else P, lo:hi] = value
    p = np.arange(P)
    put("ident", np.eye(P))
    put("tri", p[:, None] < p[None, :])
    put("ones", np.ones((P, P)))
    put("mask", (p[:, None, None] // DH + 2 * np.arange(CH)[None, :, None] == np.arange(H)[None, None, :]))
    put("iota", np.arange(E)[None])
    put("dest", p[:, None, None] + P * np.arange(TILES)[None, :, None] + N * np.arange(TOPK)[None, None, :])
    put("first", (REGION * np.arange(E))[None])
    put("block", np.arange(NBLK)[None])
    put("step", np.broadcast_to(BLK * np.arange(16)[None, :], (E, 16)).reshape(1, -1))
    put("upto", (np.arange(E)[None, :] <= np.arange(E)[:, None]).reshape(1, -1))
    return c



def program(nc, x, xT, wqkvT, wf, bf, wout, bout, gwT, w12, consts, out):
    ctx = ExitStack()
    with ctx:
        def sb(name, shape, dt=F32):
            return ctx.enter_context(nc.sbuf_tensor(name, shape, dt))

        def pb(name, shape, dt=F32):
            return ctx.enter_context(nc.psum_tensor(name, shape, dt))

        def sem(name):
            return ctx.enter_context(nc.semaphore(name))

        xs = nc.dram_tensor("expert_rows", [XS_ROWS, ROW], F32, kind="Internal").ap()
        ys = nc.dram_tensor("expert_results", [TOPK * N, D], F32, kind="Internal").ap()

        cst = sb("cst", [P, C_COLS])

        def con(name, rows=P):
            lo, hi = _C[name]
            return cst[0:rows, lo:hi]
        x_raw = sb("x_raw", [P, B * TILES, D])
        xT_raw = sb("xT_raw", [P, N + S])
        x1 = sb("x1", [P, B * TILES, D])
        wq_hi, wq_lo = sb("wq_hi", [P, HD], F32R), sb("wq_lo", [P, HD], F32R)
        wk_hi, wk_lo = sb("wk_hi", [P, HD], F32R), sb("wk_lo", [P, HD], F32R)
        vo_hi, vo_lo = sb("vo_hi", [P, H * D], F32R), sb("vo_lo", [P, H * D], F32R)
        xT_hi, xT_lo = sb("xT_hi", [P, S], F32R), sb("xT_lo", [P, S], F32R)
        x_hi, x_lo = sb("x_hi", [P, TILES, D], F32R), sb("x_lo", [P, TILES, D], F32R)
        k_hi, k_lo = sb("k_hi", [P, TILES, HD], F32R), sb("k_lo", [P, TILES, HD], F32R)
        q_act = sb("q_act", [P, CH, S])
        g_hi, g_lo = sb("g_hi", [P, HD], F32R), sb("g_lo", [P, HD], F32R)
        m_hi, m_lo = sb("m_hi", [P, CH, D], F32R), sb("m_lo", [P, CH, D], F32R)
        qn = sb("qn", [P, 4, S])
        qn_hi, qn_lo = sb("qn_hi", [P, 2, S], F32R), sb("qn_lo", [P, 2, S], F32R)
        rows = sb("rows", [P, TILES, TOPK, ROW])
        zeros = sb("zeros", [P, BLK // P, ROW])
        warm = sb("warm", [P, 2])
        wfd = sb("wfd", [P, P])
        bf_col = sb("bf_col", [P, 1])
        bout_col = sb("bout_col", [P, 1])
        gw = sb("gw", [P, E])
        gwc = sb("gwc", [P, E])
        ones_r = sb("ones_r", [P, H], F32R)
        ones_b = sb("ones_b", [P, P], BF16)
        tri_b = sb("tri_b", [P, P], BF16)
        bf_rows = sb("bf_rows", [3, S], BF16)
        ksd = sb("ksd", [P, CH, H])
        rn = sb("rn", [H, 2, S])
        r_bc = sb("r_bc", [P, R_RING, S])
        stats = sb("stats", [P, B * TILES, 6])
        mv = sb("mv", [P, B * TILES, 2])
        ln = sb("ln", [P, 4, B * TILES])
        logit = sb("logit", [P, TILES, E])
        top = sb("top", [P, TILES, 8])
        topi = sb("topi", [P, TILES, 8], U32)
        topd = sb("topd", [P, TILES, 8])
        tope = sb("tope", [P, TILES, 8])
        den = sb("den", [P, 2, TILES])
        topf = sb("topf", [P, TILES, TOPK])
        hot = sb("hot", [P, TILES, TOPK, E])
        hot_sum = sb("hot_sum", [P, TILES + 1, E], BF16)
        rank = sb("rank", [P, TILES, E])
        picked = sb("picked", [P, TILES, TOPK, E])
        posf = sb("posf", [P, TILES, TOPK])
        pos = sb("pos", [P, TILES, TOPK], I32)
        base = sb("base", [P, E])
        dest = sb("dest", [P, TILES, TOPK])
        cnt = sb("cnt", [1, 3, E])
        full = sb("full", [1, E, 16])
        upto_n = sb("upto_n", [1, E, E])
        endi = sb("endi", [1, E], I32)
        tab = sb("tab", [1, 5, NBLK])
        tabi = sb("tabi", [1, 2, NBLK], I32)
        wqkvT_sb = q_act[:, :, :].rearrange("p c s -> p (c s)")[:, 0:3 * HD].rearrange("p (c d) -> p c d", d=D)
        q_space = q_act[:, :, :].rearrange("p c s -> p (c s)")
        woutd = x1[:, 0:2 * CH, :].rearrange("p (c a) d -> p c a d", a=2)
        zT = qn[:, 3, :]
        krow = qn[0:1, 1:3, :].rearrange("p a s -> p (a s)")
        bf_raw = rn[0:1, 0, 0:DH]
        bf_part = [rn[0:1, 1, i * DH:(i + 1) * DH].bitcast(BF16)[:, 0:DH] for i in range(3)]
        past = krow[:, 0:2 * NBLK * E].rearrange("p (a n e) -> p a n e", a=2, e=E)
        hT = [q_space[:, v * FC * BLK:(v + 1) * FC * BLK].rearrange("p (c s) -> p c s", c=FC) for v in range(2)]
        yrow = [q_space[:, 2 * FC * BLK + 2 * u * D:2 * FC * BLK + 2 * (u + 1) * D].rearrange("p (c d) -> p c d", d=D) for u in range(SLOTS)]
        w_raw = [xT_raw[:, u * W_ROW:(u + 1) * W_ROW] for u in range(3)] + [
            x_raw[:, :, :].rearrange("p c d -> p (c d)")[:, u * W_ROW:(u + 1) * W_ROW] for u in range(SLOTS - 3)]
        xrow = [rows[:, u, :, :] for u in range(TILES)] + [
            x_raw[:, :, :].rearrange("p c d -> p (c d)")[:, (SLOTS - 3) * W_ROW + u * 2 * ROW:(SLOTS - 3) * W_ROW + (u + 1) * 2 * ROW].rearrange("p (c d) -> p c d", d=ROW)
            for u in range(SLOTS - TILES)]
        w2_raw = [w[:, F + FC:W_ROW - D].rearrange("p (c n) -> p c n", c=FC) for w in w_raw]
        b2_bc = [w[:, None, W_ROW - D:].broadcast_to([P, 2, D]) for w in w_raw]
        ya = x_raw
        yb = xT_raw[:, 0:N].rearrange("p (t d) -> p t d", d=D)
        psA = pb("psA", [P, 2, 1024])
        psG = pb("psG", [P, 2, 512])
        psO = pb("psO", [P, 512])
        psS = pb("psS", [P, 512])
        psV = [psG[:, 0, :], psG[:, 1, :], psO[:, :], psS[:, :]]
        psA_m = psA[:, :, :].rearrange("p h (c a d) -> p h c a d", c=CH // 2, a=2)
        psA_k = psA[0:H, 0, :]
        psG_k = psG[:, 1, 0:2 * CH].rearrange("p (c n) -> p c n", n=2)
        psS_l = psS[:, 0:TILES * E].rearrange("p (t e) -> p t e", e=E)
        psO_z = psO[:, :].rearrange("p (t d) -> p t d", d=D)
        psO_c = psO[:, 0:(TILES + 1) * E].rearrange("p (t e) -> p t e", e=E)
        psX = [psG[:, v, 0:BLK] for v in range(2)]
        psH = [psA[:, v, :].rearrange("p (c s) -> p c s", c=FC) for v in range(2)]
        psY = [ps[:, 0:2 * D].rearrange("p (t d) -> p t d", d=D) for ps in (psO, psS)]

        psZ = [psA[:, g // 2, g % 2 * 512:(g % 2 + 1) * 512] for g in range(4)] + [psG[:, 0, :], psG[:, 1, :]] + \
            ([psO[:, :], psS[:, :]] if NBLK % 2 == 0 else [psS[:, :], psO[:, :]])
        psZ_t = [z[:, t * D:(t + 1) * D] for z in psZ for t in range(TILES)]

        in_c, in_fold, in_x0, in_x, in_small, in_bias = (sem(n) for n in ("in_c", "in_fold", "in_x0", "in_x", "in_small", "in_bias"))
        cleared, zero_ready, filled, bf_in = (sem(n) for n in ("cleared", "zero_ready", "filled", "bf_in"))
        cast, bias_step, fold_pe, fold_hi, fold_lo, mean_pe, gwc_ready = (
            sem(n) for n in ("cast", "bias_step", "fold_pe", "fold_hi", "fold_lo", "mean_pe", "gwc_ready"))
        xT_h, xT_l, x_h, x_l = (sem(n) for n in ("xT_h", "xT_l", "x_h", "x_l"))
        k_pe, k_h, k_l, q_pe, q_done, g_pe, g_h, g_l, m_pe, m_h, m_l = (
            sem(n) for n in ("k_pe", "k_h", "k_l", "q_pe", "q_done", "g_pe", "g_h", "g_l", "m_pe", "m_h", "m_l"))
        ks_pe, krow_done, ksT_pe, ks_done, n_pe, n_step, qn_done, qn_h, qn_l, o_pe, zT_done = (
            sem(n) for n in ("ks_pe", "krow_done", "ksT_pe", "ks_done", "n_pe", "n_step", "qn_done", "qn_h", "qn_l", "o_pe", "zT_done"))
        z_pe, l_pe, c_pe, st_step, ln_step, x1_done, route, exp_done, scattered, table = (
            sem(n) for n in ("z_pe", "l_pe", "c_pe", "st_step", "ln_step", "x1_done", "route", "exp_done", "scattered", "table"))
        e_x, e_w, e_out = ([sem(f"{n}{u}") for u in range(SLOTS)] for n in ("e_x", "e_w", "e_out"))
        e_T, e_Th, e_Tl, e_wh, e_wl, e_up, e_gelu, e_down, e_y0, e_y1, e_y = (
            sem(n) for n in ("e_T", "e_Th", "e_Tl", "e_wh", "e_wl", "e_up", "e_gelu", "e_down", "e_y0", "e_y1", "e_y"))
        in_xr0, in_fold_v, m_h0, m_l0, tab_step = (sem(n) for n in ("in_xr0", "in_fold_v", "m_h0", "m_l0", "tab_step"))
        r_in = [sem(f"r_in{j}") for j in range(R_RING)]
        warmed, ends, padded = sem("warmed"), sem("ends"), sem("padded")
        qn_lp = sem("qn_lp")
        f_in, f_out = ([sem(f"{n}{g}") for g in range(B)] for n in ("f_in", "f_out"))
        f_norm_dve = sem("f_norm_dve")
        f_z, f_stats, f_ln, f_norm = (sem(n) for n in ("f_z", "f_stats", "f_ln", "f_norm"))

        N_STEPS, LN_STEPS, ST_STEPS, ROUTE_STEPS = 3, 12, 2 * TILES, 24
        TOP_AT, HOT_AT = 10, 13

        class Steps:

            def __init__(self, eng, which, done):
                self.eng, self.which, self.n = eng, which, done

            def __call__(self, ins):
                ins.then_inc(self.which, 1)
                self.n = self.n + 1

            def wait(self):
                self.eng.wait_ge(self.which, self.n)

        def wait_alone(eng, which, value):
            eng.wait_ge(which, value)
            eng.nop(nofuse=True)

        def batches(eng, body):
            body(0, False, True)
            body(1, True, True)
            with eng.Fori(2, B) as b:
                body(b, True, True)
            body(B, True, False)

        def blocks(eng, body):
            for u in range(SLOTS):
                body(u, u, 0)
            with eng.Fori(1, NBLK // SLOTS) as i:
                for u in range(SLOTS):
                    body(SLOTS * i + u, u, i)
            for u in range(NBLK % SLOTS):
                body(NBLK // SLOTS * SLOTS + u, u, NBLK // SLOTS)

        def earlier(n, u, i, back):
            return n - back, (u - back) % SLOTS, i - (u < back)

        last_blocks = [(n, n % SLOTS, n // SLOTS) for n in (NBLK - 2, NBLK - 1)]

        def later(n, least):
            return not isinstance(n, int) or n >= least

        LAST = 2
        groups = [(g, slice(g * TILES, (g + 1) * TILES)) for g in range(B)]

        block = ctx.enter_context(nc.Block())

        @block.sync
        def _(sp):
            wqkv_v = wqkvT.rearrange("(c p) d -> p c d", p=P)
            sp.dma_start(wqkvT_sb[:, 0:2 * CH, :], wqkv_v[:, 0:2 * CH, :]).then_inc(in_fold, 16)
            sp.wait_ge(cleared, 1)
            for r in (0, DH):
                sp.dma_start(wfd[r:r + DH, r:r + DH], wf).then_inc(in_fold, 16)
            x_v = x.rearrange("(t p) d -> p t d", p=P)
            sp.dma_start(xT_raw[:, 0:S], xT[:, 0:S]).then_inc(in_x0, 16)
            sp.dma_start(wqkvT_sb[:, 2 * CH:, :], wqkv_v[:, 2 * CH:, :]).then_inc(in_fold_v, 16)
            sp.wait_ge(cleared, 2)
            wout_v = wout.rearrange("(c a p) n -> a p c n", a=2, p=DH)
            for a in range(2):
                sp.dma_start(woutd[DH * a:DH * a + DH, :, a, :], wout_v[a]).then_inc(in_fold_v, 16)
            sp.dma_start(x_raw[:, 0:TILES, :], x_v[:, 0:TILES, :]).then_inc(in_xr0, 16)
            sp.wait_ge(bias_step, 5)
            for i in range(3):
                sp.dma_start(bf_rows[i:i + 1, :].rearrange("p (h d) -> p h d", d=DH),
                             bf_part[i][:, None, :].broadcast_to([1, S // DH, DH])).then_inc(bf_in, 16)
            sp.dma_start(xT_raw[:, S:N], xT[:, S:]).then_inc(in_x, 16)
            sp.dma_start(x_raw[:, TILES:, :], x_v[:, TILES:, :]).then_inc(in_x, 16)
            sp.wait_ge(zero_ready, 2)
            sp.dma_start(xs[NOWHERE:NOWHERE + BLK, :].rearrange("(p f) c -> p f c", p=P), zeros[:, :, :]).then_inc(filled, 16)

            def spread(b, prev, cur):
                if not prev:
                    return
                wait_alone(sp, n_step, N_STEPS * b)
                for c in range(CH):
                    if c >= R_RING or not (isinstance(b, int) and b == 1):
                        wait_alone(sp, qn_done, CH * (b - 1) + c - R_RING + 1)
                    for a in range(2):
                        sp.dma_start(r_bc[DH * a:DH * (a + 1), c % R_RING, :],
                                     rn[2 * c + a:2 * c + a + 1, 1, :][:, None, :].broadcast_to([1, DH, S])).then_inc(r_in[c % R_RING], 16)
            batches(sp, spread)

            sp.wait_ge(ends, 1)
            for e in range(E):
                end = sp.value_load(endi[0:1, e:e + 1], min_val=e * REGION, max_val=(e + 1) * REGION - S - BLK)
                sp.dma_start(xs[ds(end, S + BLK), :].rearrange("(p r f) c -> p r (f c)", p=P, f=BLK // P),
                             zeros[:, :, :].rearrange("p f c -> p (f c)")[:, None, :]
                             .broadcast_to([P, (S + BLK) // BLK, BLK // P * ROW])).then_inc(padded, 16)

            sp.wait_ge(table, 2)

            def load_weights(n, u):
                expert = sp.value_load(tabi[0:1, 0, ds(n, 1)], min_val=0, max_val=E - 1)
                sp.dma_start(w_raw[u], w12[ds(expert, 1), :, :].rearrange("a p n -> (a p) n")).then_inc(e_w[u], 16)

            def load_rows(n, u):
                first = sp.value_load(tabi[0:1, 1, ds(n, 1)], min_val=0, max_val=NOWHERE)
                sp.dma_start(xrow[u], xs[ds(first, BLK), :].rearrange("(c p) d -> p c d", p=P)).then_inc(e_x[u], 16)

            for u in range(2):
                load_weights(u, u)
            sp.wait_ge(filled, 16)
            sp.wait_ge(scattered, 16 * TILES * TOPK * B)
            for u in range(2):
                load_rows(u, u)
            for u in range(2, SLOTS):
                load_weights(u, u)
                load_rows(u, u)

            def load(n, u, i):
                if isinstance(n, int) and n < SLOTS:
                    return
                wait_alone(sp, e_y, n - SLOTS + 1)
                load_weights(n, u)
                wait_alone(sp, e_out[u], 32 * i)
                load_rows(n, u)
            blocks(sp, load)

            for u in range(SLOTS):
                sp.wait_ge(e_out[u], 32 * ((NBLK - u + SLOTS - 1) // SLOTS))
            ya_v = ys[0:N, :].rearrange("(t p) d -> p t d", p=P)
            yb_v = ys[N:2 * N, :].rearrange("(t p) d -> p t d", p=P)

            for g, at in groups:
                sp.dma_start(ya[:, at, :], ya_v[:, at, :]).then_inc(f_in[g], 16)
                sp.dma_start(yb[:, at, :], yb_v[:, at, :]).then_inc(f_in[g], 16)
            out_v = out.rearrange("b (t p) d -> p (b t) d", p=P)
            for g, at in groups:
                if g < B - LAST:
                    sp.wait_ge(f_norm, TILES * (g + 1))
                else:
                    sp.wait_ge(f_norm_dve, TILES * (g - B + LAST + 1))
                sp.dma_start(out_v[:, at, :], yb[:, at, :]).then_inc(f_out[g], 16)
            for g in range(B):
                sp.wait_ge(f_out[g], 16)

        @block.gpsimd
        def _(pool):
            pool.memset(wfd[:, :], 0.0).then_inc(cleared, 1)
            pool.memset(x1[:, 0:2 * CH, :], 0.0).then_inc(cleared, 1)
            pool.memset(xT_raw[:, N:], 0.0)

            def low(out_, full_, hi_):
                return pool.tensor_tensor(out_, full_, hi_.bitcast(F32), ALU.subtract)

            def scatter(b, prev, cur):
                if prev:
                    for c in range(1, CH, 2):
                        pool.wait_ge(qn_h, CH * (b - 1) + c + 1)
                        low(qn_lo[:, c % 2, :], qn[:, c % 4, :], qn_hi[:, c % 2, :]).then_inc(qn_lp, 1)
                if cur:
                    pool.wait_ge(x_h, b + 1)
                    low(x_lo[:, :, :], x_raw[:, ds(b * TILES, TILES), :], x_hi[:, :, :]).then_inc(x_l, 1)
                    pool.wait_ge(xT_h, b + 2)
                    low(xT_lo[:, :], xT_raw[:, ds((b + 1) * S, S)], xT_hi[:, :]).then_inc(xT_l, 1)
                if not prev:
                    return
                if not cur:
                    pool.wait_ge(padded, 16 * E)
                wait_alone(pool, route, ROUTE_STEPS * b)
                for j in range(TILES):
                    for k in range(TOPK):
                        pool.indirect_dma_start(xs, bass.IndirectOffsetOnAxis(ap=pos[:, j, k:k + 1], axis=0),
                                                rows[:, j, k, :], None).then_inc(scattered, 16)
            pool.wait_ge(xT_h, 1)
            low(xT_lo[:, :], xT_raw[:, 0:S], xT_hi[:, :]).then_inc(xT_l, 1)
            batches(pool, scatter)

            def store(n, u, i):
                wait_alone(pool, e_y, n + 1)
                for c in range(2):
                    pool.indirect_dma_start(ys, bass.IndirectOffsetOnAxis(ap=xrow[u][:, c, D:D + 1].bitcast(I32), axis=0),
                                            yrow[u][:, c, :], None, bounds_check=TOPK * N - 1, oob_is_err=False).then_inc(e_out[u], 16)
            blocks(pool, store)

        @block.tensor
        def _(pe):
            mm = pe.matmul

            def three(outp, a_hi, a_lo, b_hi, b_lo, start=True, stop=True):
                mm(outp, a_hi, b_hi, start=start, stop=False)
                mm(outp, a_hi, b_lo, start=False, stop=False)
                return mm(outp, a_lo, b_hi, start=False, stop=stop)

            pe.wait_ge(in_fold, 48)
            for part in (1, 0):
                for c in range(CH):
                    last = mm(psA[:, part, c * P:(c + 1) * P], wqkvT_sb[:, part * CH + c, :], wfd[:, :], start=True, stop=True)
                last.then_inc(fold_pe, 1)
            pe.wait_ge(in_fold_v, 48)
            for cc in range(CH):
                last = mm(psV[cc // 2][:, (cc % 2) * 256:(cc % 2 + 1) * 256], wqkvT_sb[:, 2 * CH + cc, :], woutd[:, cc, :, :], start=True, stop=True)
                if cc in (3, 5, 7):
                    last.then_inc(fold_pe, 1)
            pe.wait_ge(in_c, 16)
            pe.wait_ge(in_small, 64)
            pe.wait_ge(fold_lo, 2)
            mm(psA[:, 0, 0:E], con("ones"), gw[:, :], start=True, stop=True).then_inc(mean_pe, 1)
            pe.wait_ge(cast, 7)
            pe.wait_ge(bf_in, 48)
            pe.wait_ge(gwc_ready, 1)
            def attention(b, prev, cur):
                def output(c):
                    if c == 0:
                        pe.wait_ge(m_l, 2 * b)
                        pe.wait_ge(route, ROUTE_STEPS * (b - 1))
                    pe.wait_ge(qn_lp if c % 2 else qn_l, CH // 2 * (b - 1) + c // 2 + 1)
                    three(psO[:, :], m_hi[:, c, :], m_lo[:, c, :], qn_hi[:, c % 2, :], qn_lo[:, c % 2, :],
                          start=c == 0, stop=c == CH - 1).then_inc(o_pe, 1)

                def keys(t):
                    if t == 0:
                        pe.wait_ge(xT_l, b + 1)
                    if t < 2 and prev:
                        pe.wait_ge(m_l, 2 * b - 1 + t)
                    if t >= 2:
                        pe.wait_ge(k_l, TILES * b + t - 1)
                    at = slice(t * P, (t + 1) * P)
                    for h in range(2):
                        to = psA[:, t % 2, h * 512:(h + 1) * 512]
                        cols = slice(h * 512, (h + 1) * 512)
                        mm(to, ones_b[0:3, :], bf_rows[:, :], start=True, stop=False)
                        mm(to, xT_hi[:, at], wk_hi[:, cols], start=False, stop=False)
                        mm(to, xT_hi[:, at], wk_lo[:, cols], start=False, stop=False)
                        last = mm(to, xT_lo[:, at], wk_hi[:, cols], start=False, stop=True)
                    last.then_inc(k_pe, 1)

                def queries(i):
                    if i < 2:
                        pe.wait_ge(k_l, TILES * b + i + 3)
                    elif i == 2:
                        pe.wait_ge(q_done, CH // 2 * b + 2)
                    else:
                        pe.wait_ge(krow_done, b + 1)
                    for j in range(2):
                        c = 2 * i + j
                        at = slice(c * P, (c + 1) * P)
                        last = three(psA[:, (i + i // 2) % 2, j * 512:(j + 1) * 512], wq_hi[:, at], wq_lo[:, at], xT_hi[:, :], xT_lo[:, :])
                    last.then_inc(q_pe, 1)

                def logits():
                    pe.wait_ge(zT_done, b)
                    for j in range(TILES):
                        last = mm(psS_l[:, j, :], zT[:, j * P:(j + 1) * P], gwc[:, :], start=True, stop=True)
                    last.then_inc(l_pe, 1)
                    for j in range(TILES):
                        last = pe.transpose(psO_z[:, j, :], zT[:, j * P:(j + 1) * P], con("ident"))
                    last.then_inc(z_pe, 1)

                def ranks():
                    pe.wait_ge(x1_done, TILES * b)
                    pe.wait_ge(route, ROUTE_STEPS * (b - 1) + HOT_AT)
                    mm(psO_c[:, :, :], tri_b[:, :], hot_sum[:, :, :], start=True, stop=False)
                    for j in range(TILES):
                        last = mm(psO_c[:, j + 1:, :], ones_b[:, :], hot_sum[:, j:j + 1, :].broadcast_to([P, TILES - j, E]),
                                  start=False, stop=j == TILES - 1)
                    last.then_inc(c_pe, 1)

                def sums():
                    pe.wait_ge(q_done, CH // 2 * b + 1)
                    pe.wait_ge(k_l, TILES * (b + 1))
                    for h in range(2):
                        cols = slice(h * 512, (h + 1) * 512)
                        for t in range(TILES):
                            mm(psA_k[:, cols], ones_r[:, :], k_hi[:, t, cols], start=t == 0, stop=False)
                            last = mm(psA_k[:, cols], ones_r[:, :], k_lo[:, t, cols], start=False, stop=t == TILES - 1)
                    last.then_inc(ks_pe, 1)

                def turn_sums():
                    pe.wait_ge(krow_done, b + 1)
                    if prev:
                        pe.wait_ge(g_l, 2 * b)
                    for c in range(CH):
                        last = mm(psG_k[:, c, :], krow[0:1, c * P:(c + 1) * P], con("ones", 1)[:, 0:2], start=True, stop=True)
                    last.then_inc(ksT_pe, 1)

                def gram(h):
                    if h == 0:
                        pe.wait_ge(x_l, b + 1)
                    else:
                        pe.wait_ge(ks_done, b + 1)
                    cols = slice(h * 512, (h + 1) * 512)
                    for t in range(TILES):
                        last = three(psG[:, h, :], x_hi[:, t, :], x_lo[:, t, :], k_hi[:, t, cols], k_lo[:, t, cols],
                                     start=t == 0, stop=t == TILES - 1)
                    last.then_inc(g_pe, 1)

                def norms():
                    pe.wait_ge(ks_done, b + 1)
                    pe.wait_ge(q_done, CH // 2 * b + 3)
                    if prev:
                        pe.wait_ge(route, ROUTE_STEPS * (b - 1) + 1)
                    for c in range(CH):
                        if c == 6:
                            pe.wait_ge(q_done, CH // 2 * (b + 1))
                        last = mm(psS[0:H, :], ksd[:, c, :], q_act[:, c, :], start=c == 0, stop=c == CH - 1)
                    last.then_inc(n_pe, 1)

                def mix(half):
                    pe.wait_ge(g_l, 2 * b + half + 1)
                    for i in range(CH // 2):
                        c = half * CH // 2 + i
                        at, cols = slice(c * P, (c + 1) * P), slice(2 * c * D, 2 * (c + 1) * D)
                        last = three(psA[:, half, i * 256:(i + 1) * 256], g_hi[:, at], g_lo[:, at], vo_hi[:, cols], vo_lo[:, cols])
                    last.then_inc(m_pe, 1)

                if cur:
                    keys(0)
                if cur:
                    keys(1)
                for t in range(TILES):
                    if prev:
                        output(2 * t)
                        output(2 * t + 1)
                    if cur:
                        (keys if t < 2 else queries)((t + 2) % TILES)
                if prev:
                    logits()
                if cur:
                    sums()
                    queries(2)
                    turn_sums()
                    queries(3)
                    norms()
                if prev:
                    ranks()
                if cur:
                    gram(0)
                    gram(1)
                    mix(0)
                    mix(1)
            batches(pe, attention)

            def turn_rows(n, u, i):
                pe.wait_ge(e_x[u], 16 * i + 16)
                if later(n, 2):
                    pe.wait_ge(e_Tl, n - 1)
                for c in range(2):
                    last = pe.transpose(psX[u % 2][:, c * P:(c + 1) * P], xrow[u][:, c, 0:D], con("ident"))
                last.then_inc(e_T, 1)

            def first_layer(n, u, i):
                v = u % 2
                pe.wait_ge(e_Tl, n + 1)
                pe.wait_ge(e_wl, n + 1)
                if later(n, 2):
                    pe.wait_ge(e_gelu, FC * (n - 1))
                at = slice(v * BLK, (v + 1) * BLK)
                for c in range(FC):
                    w = slice(v * F + c * P, v * F + (c + 1) * P)
                    last = three(psH[v][:, c, :], wq_hi[:, w], wq_lo[:, w], xT_hi[:, at], xT_lo[:, at])
                    last.then_inc(e_up, 1)

            def second_layer(n, u, i):
                v = u % 2
                pe.wait_ge(e_gelu, FC * (n + 1))
                if later(n, 2):
                    pe.wait_ge(e_y0, n - 1)
                for t in range(2):
                    for c in range(FC):
                        last = mm(psY[v][:, t, :], hT[v][:, c, t * P:(t + 1) * P], w2_raw[u][:, c, :], start=c == 0, stop=c == FC - 1)
                last.then_inc(e_down, 1)

            def experts(n, u, i):
                turn_rows(n, u, i)
                if later(n, 1):
                    first_layer(*earlier(n, u, i, 1))
                if later(n, 2):
                    second_layer(*earlier(n, u, i, 2))
            blocks(pe, experts)
            first_layer(*last_blocks[1])
            second_layer(*last_blocks[0])
            second_layer(*last_blocks[1])

            for g, at in groups:
                if g >= B - 2:
                    pe.wait_ge(e_y0, NBLK - (B - 1 - g))
                mm(psZ[g], con("ident"), x1[:, at, :].rearrange("p t d -> p (t d)"), start=True, stop=False)
            for g, at in groups:
                pe.wait_ge(f_in[g], 32)
                mm(psZ[g], con("ident"), ya[:, at, :].rearrange("p t d -> p (t d)"), start=False, stop=False)
                mm(psZ[g], con("ident"), yb[:, at, :].rearrange("p t d -> p (t d)"), start=False, stop=True).then_inc(f_z, 1)

        @block.scalar
        def _(act):
            def hi(out_, in_, func=ACT.Copy, **kw):
                return act.activation(out_, in_, func, **kw)

            act.dma_start(bf_raw, bf[None, :]).then_inc(in_bias, 16)
            act.dma_start(cst[:, :], consts[:, 0:C_COLS]).then_inc(in_c, 16)
            act.dma_start(gw[:, :], gwT).then_inc(in_small, 16)
            act.dma_start(bout_col[:, :], bout.rearrange("(d a) -> d a", a=1)).then_inc(in_small, 16)
            act.dma_start(bf_col[0:DH, :], bf.rearrange("(d a) -> d a", a=1)).then_inc(in_small, 16)
            act.dma_start(bf_col[DH:P, :], bf.rearrange("(d a) -> d a", a=1)).then_inc(in_small, 16)
            act.wait_ge(zero_ready, 1)
            act.activation(warm[:, 0:1], zeros[:, 0, 0:1], ACT.Copy).then_inc(warmed, 1)
            act.wait_ge(in_x0, 16)
            hi(xT_hi[:, :], xT_raw[:, 0:S]).then_inc(xT_h, 1)
            for i, (to, src) in enumerate(((wk_hi[:, :], psA[:, 1, :]), (wq_hi[:, :], psA[:, 0, :]),
                                           (vo_hi[:, 0:1024], psG[:, :, :].rearrange("p a s -> p (a s)")),
                                           (vo_hi[:, 1024:1536], psO[:, :]), (vo_hi[:, 1536:], psS[:, :]))):
                act.wait_ge(fold_pe, i + 1)
                hi(to, src).then_inc(fold_hi, 1)

            def attention(b, prev, cur):
                def out_hi(c):
                    act.wait_ge(qn_done, CH * (b - 1) + c + 1)
                    act.wait_ge(o_pe, CH * (b - 1) + max(c - 1, 0))
                    hi(qn_hi[:, c % 2, :], qn[:, c % 4, :]).then_inc(qn_h, 1)

                def key_hi(t):
                    act.wait_ge(k_pe, TILES * b + t + 1)
                    if t == 0:
                        act.wait_ge(g_pe, 2 * b)
                        act.wait_ge(ks_pe, b)
                    hi(k_hi[:, t, :], psA[:, t % 2, :], ACT.Relu).then_inc(k_h, 1)

                def query(i):
                    act.wait_ge(q_pe, CH // 2 * b + i + 1)
                    if prev:
                        act.wait_ge(n_pe, b)
                        act.wait_ge(qn_done, CH * (b - 1) + 2 * i + 2)
                    hi(q_act[:, 2 * i:2 * i + 2, :], psA[:, (i + i // 2) % 2, :].rearrange("p (c s) -> p c s", c=2), ACT.Relu,
                       bias=bf_col[:, 0:1]).then_inc(q_done, 1)

                for t in range(TILES):
                    if prev:
                        out_hi(2 * t)
                        out_hi(2 * t + 1)
                    if cur and t == 0:
                        key_hi(0)
                    if cur:
                        if t + 1 < TILES:
                            key_hi(t + 1)
                        else:
                            query(0)
                if cur:
                    query(1)
                    if not prev:
                        act.wait_ge(in_xr0, 16)
                    act.wait_ge(g_pe, 2 * b)
                    hi(x_hi[:, :, :], x_raw[:, ds(b * TILES, TILES), :]).then_inc(x_h, 1)
                    act.wait_ge(ks_pe, b + 1)
                    if prev:
                        act.wait_ge(o_pe, CH * b)
                    hi(krow[:, :], psA_k[0:1, :]).then_inc(krow_done, 1)
                    query(2)
                    query(3)
                if prev:
                    act.wait_ge(ln_step, LN_STEPS * b)
                    for j in range(TILES):
                        act.activation(x1[:, ds((b - 1) * TILES + j, 1), :], psO_z[:, j:j + 1, :], ACT.Identity,
                                       bias=ln[:, 3, j:j + 1], scale=ln[:, 1, j:j + 1]).then_inc(x1_done, 1)
                    act.wait_ge(route, ROUTE_STEPS * (b - 1) + TOP_AT)
                    act.activation(tope[:, :, :], topd[:, :, :], ACT.Exp).then_inc(exp_done, 1)
                if cur:
                    if isinstance(b, int) and b == 0:
                        act.wait_ge(in_x, 32)
                    act.wait_ge(q_pe, CH // 2 * (b + 1))
                    hi(xT_hi[:, :], xT_raw[:, ds((b + 1) * S, S)]).then_inc(xT_h, 1)
                    for h in range(2):
                        act.wait_ge(g_pe, 2 * b + h + 1)
                        if h == 0:
                            act.wait_ge(m_pe, 2 * b)
                        hi(g_hi[:, h * 512:(h + 1) * 512], psG[:, h, :]).then_inc(g_h, 1)
                    for h in range(2):
                        act.wait_ge(m_pe, 2 * b + h + 1)
                        if h == 0:
                            act.wait_ge(o_pe, CH * b)
                        for a in range(2):
                            r = slice(DH * a, DH * (a + 1))
                            hi(m_hi[r, h * CH // 2:(h + 1) * CH // 2, :], psA_m[r, h, :, a, :]).then_inc((m_h0, m_h)[a], 1)
            batches(act, attention)
            act.wait_ge(xT_l, B + 1)
            act.activation(warm[:, 1:2], zeros[:, 0, 0:1], ACT.Gelu_apprx_tanh).then_inc(warmed, 1)

            def gelu(n, u, i):
                v = u % 2
                act.wait_ge(e_w[u], 16 * i + 16)
                for c in range(FC):
                    act.wait_ge(e_up, FC * n + c // 2 * 2 + 2)
                    if c == 0 and later(n, 2):
                        act.wait_ge(e_down, n - 1)
                    act.activation(hT[v][:, c, :], psH[v][:, c, :], ACT.Gelu_apprx_tanh,
                                   bias=w_raw[u][:, F + c:F + c + 1]).then_inc(e_gelu, 1)

            def experts(n, u, i):
                act.wait_ge(e_T, n + 1)
                if later(n, 2):
                    act.wait_ge(e_up, FC * (n - 1))
                v = u % 2
                hi(xT_hi[:, v * BLK:(v + 1) * BLK], psX[v]).then_inc(e_Th, 1)
                if later(n, 1):
                    gelu(*earlier(n, u, i, 1))
            blocks(act, experts)
            gelu(*last_blocks[1])


            act.wait_ge(f_ln, LN_STEPS)
            for t in range((B - LAST) * TILES):
                act.activation(yb[:, t, :], psZ_t[t], ACT.Identity,
                               bias=ln[:, 3, t:t + 1], scale=ln[:, 1, t:t + 1]).then_inc(f_norm, 1)

        @block.vector
        def _(dve):
            def lo(out_, full_, hi_):
                return dve.tensor_tensor(out_, full_, hi_.bitcast(F32), ALU.subtract)

            def norm_steps(step, cols):
                v, y, t, nb = (ln[:, i, cols] for i in range(4))
                step(dve.tensor_scalar(v, mv[:, cols, 1], LN_EPS, None, ALU.add))
                step.wait()
                step(dve.tensor_scalar(y.bitcast(I32), v.bitcast(I32), -0.5, RSQRT_SEED, ALU.mult, ALU.add))
                for _ in range(3):
                    step.wait()
                    step(dve.tensor_tensor(t, y, y, ALU.mult))
                    step.wait()
                    step(dve.scalar_tensor_tensor(t, t, -0.5, v, ALU.mult, ALU.mult))
                    step.wait()
                    step(dve.scalar_tensor_tensor(y, t, 1.5, y, ALU.add, ALU.mult))
                step.wait()
                step(dve.scalar_tensor_tensor(nb, mv[:, cols, 0], -1.0, y, ALU.mult, ALU.mult))

            dve.memset(zeros[:, :, :], 0.0).then_inc(zero_ready, 1)
            dve.wait_ge(zero_ready, 1)
            dve.memset(zeros[:, :, D:D + 1].bitcast(I32), 65535).then_inc(zero_ready, 1)
            dve.memset(rows[:, :, :, :], 0.0).then_inc(cast, 1)
            dve.memset(hot_sum[:, :, :], 0.0).then_inc(cast, 1)
            dve.wait_ge(in_c, 16)
            dve.tensor_copy(ones_r[:, :], con("ones")[:, 0:H]).then_inc(cast, 1)
            dve.tensor_copy(ones_b[:, :], con("ones")).then_inc(cast, 1)
            dve.tensor_copy(tri_b[:, :], con("tri")).then_inc(cast, 1)
            dve.tensor_copy(base[:, :], con("first")).then_inc(cast, 1)
            dve.tensor_copy(dest[:, :, :], con("dest").rearrange("p (t k) -> p t k", k=TOPK)).then_inc(cast, 1)
            dve.wait_ge(in_bias, 16)
            step = Steps(dve, bias_step, 0)
            for i in range(3):
                step(dve.tensor_copy(bf_part[i], bf_raw))
                step.wait()
                if i < 2:
                    step(dve.tensor_tensor(bf_raw, bf_raw, bf_part[i], ALU.subtract))
                    step.wait()
            folded = [(wk_hi[:, :], wk_lo[:, :], psA[:, 1, :]), (wq_hi[:, :], wq_lo[:, :], psA[:, 0, :]),
                      (vo_hi[:, 0:1024], vo_lo[:, 0:1024], psG[:, :, :].rearrange("p a s -> p (a s)")),
                      (vo_hi[:, 1024:1536], vo_lo[:, 1024:1536], psO[:, :]), (vo_hi[:, 1536:], vo_lo[:, 1536:], psS[:, :])]
            for i, (h_, l_, src) in enumerate(folded):
                dve.wait_ge(fold_hi, i + 1)
                lo(l_, src, h_).then_inc(fold_lo, 1)
                if i == 1:
                    dve.wait_ge(mean_pe, 1)
                    dve.wait_ge(in_small, 64)
                    dve.scalar_tensor_tensor(gwc[:, :], psA[:, 0, 0:E], -1.0 / D, gw[:, :], ALU.mult, ALU.add).then_inc(gwc_ready, 1)

            def attention(b, prev, cur):
                def normalise(c):
                    dve.wait_ge(r_in[c % R_RING], 32 * ((b - 1) * (CH // R_RING) + c // R_RING + 1))
                    if c >= 4 and c % 2:
                        dve.wait_ge(qn_lp, CH // 2 * (b - 1) + c // 2 - 1)
                    elif c >= 4:
                        dve.wait_ge(qn_l, CH // 2 * (b - 1) + c // 2 - 1)
                    dve.tensor_tensor(qn[:, c % 4, :], q_act[:, c, :], r_bc[:, c % R_RING, :], ALU.mult).then_inc(qn_done, 1)

                def out_lo(c):
                    dve.wait_ge(qn_h, CH * (b - 1) + c + 1)
                    lo(qn_lo[:, c % 2, :], qn[:, c % 4, :], qn_hi[:, c % 2, :]).then_inc(qn_l, 1)

                def key_lo(t):
                    dve.wait_ge(k_h, TILES * b + t + 1)
                    dve.scalar_tensor_tensor(k_lo[:, t, :], psA[:, t % 2, :], 0.0, k_hi[:, t, :].bitcast(F32),
                                             ALU.max, ALU.subtract).then_inc(k_l, 1)

                step = Steps(dve, route, ROUTE_STEPS * (b - 1))

                def choose():
                    wait_alone(dve, step.which, step.n)
                    for j in range(TILES):
                        step(dve.max(top[:, j, :], logit[:, j, :]))
                    wait_alone(dve, step.which, step.n)
                    for j in range(TILES):
                        step(dve.max_index(topi[:, j, :], top[:, j, :], logit[:, j, :]))
                    step(dve.tensor_tensor(topd[:, :, :], top[:, :, :], top[:, :, 0:1].broadcast_to([P, TILES, 8]), ALU.subtract))
                    step.wait()
                    step(dve.tensor_copy(topf[:, :, :], topi[:, :, 0:TOPK]))
                    step.wait()
                    step(dve.tensor_tensor(hot[:, :, :, :].rearrange("p t k e -> p (t k) e"),
                                           con("iota")[:, None, :].broadcast_to([P, TILES * TOPK, E]),
                                           topf[:, :, :].rearrange("p t k -> p (t k)")[:, :, None].broadcast_to([P, TILES * TOPK, E]),
                                           ALU.is_equal))
                    step.wait()
                    step(dve.tensor_tensor(hot_sum[:, 0:TILES, :], hot[:, :, 0, :], hot[:, :, 1, :], ALU.add))
                    dve.wait_ge(exp_done, b)
                    step(dve.tensor_reduce(den[:, 0, :], tope[:, :, :], AX_X, ALU.add))
                    step.wait()
                    step(dve.reciprocal(den[:, 1, :], den[:, 0, :]))
                    step.wait()
                    dve.wait_ge(scattered, 16 * TILES * TOPK * (b - 1))
                    step(dve.tensor_tensor(rows[:, :, :, D + 1], tope[:, :, 0:TOPK],
                                           den[:, 1, :][:, :, None].broadcast_to([P, TILES, TOPK]), ALU.mult))
                    step(dve.tensor_copy(rows[:, :, :, D].bitcast(I32), dest[:, :, :]))
                    step.wait()
                    step(dve.tensor_scalar(dest[:, :, :], dest[:, :, :], float(S), None, ALU.add))
                    dve.wait_ge(x1_done, TILES * b)
                    step(dve.tensor_copy(rows[:, :, :, 0:D],
                                         x1[:, ds((b - 1) * TILES, TILES), :][:, :, None, :].broadcast_to([P, TILES, TOPK, D])))

                def place():
                    dve.wait_ge(c_pe, b)
                    step(dve.tensor_tensor(rank[:, :, :], psO_c[:, 0:TILES, :], base[:, None, :].broadcast_to([P, TILES, E]), ALU.add))
                    step.wait()
                    step(dve.tensor_tensor(base[:, :], base[:, :], psO_c[:, TILES, :], ALU.add))
                    step(dve.tensor_tensor(picked[:, :, :, :], hot[:, :, :, :],
                                           rank[:, :, None, :].broadcast_to([P, TILES, TOPK, E]), ALU.mult))
                    step.wait()
                    step(dve.tensor_reduce(posf[:, :, :], picked[:, :, :, :], AX_X, ALU.add))
                    step.wait()
                    step(dve.tensor_copy(pos[:, :, :], posf[:, :, :]))

                if prev and not cur:
                    dve.wait_ge(route, ROUTE_STEPS * (b - 1))
                    dve.tensor_copy(endi[:, :], base[0:1, :]).then_inc(ends, 1)
                if prev:
                    normalise(0)
                    normalise(1)
                if cur and not prev:
                    key_lo(0)
                for t in range(TILES):
                    if prev:
                        if t < TILES - 1:
                            out_lo(2 * t)
                            normalise(2 * t + 2)
                        if cur and t == 0:
                            key_lo(0)
                        if t < TILES - 1:
                            normalise(2 * t + 3)
                        if t == TILES - 2:
                            out_lo(2 * t + 2)
                    if cur and t + 1 < TILES:
                        key_lo(t + 1)
                if prev:
                    dve.wait_ge(o_pe, CH * b)
                    dve.scalar_tensor_tensor(zT[:, :], psO[:, :], bout_col[:, 0:1], xT_raw[:, ds((b - 1) * S, S)],
                                             ALU.add, ALU.add).then_inc(zT_done, 1)
                    dve.wait_ge(z_pe, b)
                    st = Steps(dve, st_step, ST_STEPS * (b - 1))
                    for j in range(TILES):
                        st(dve.bn_stats(stats[:, j, :], psO_z[:, j, :]))
                    wait_alone(dve, st.which, st.n)
                    for j in range(TILES):
                        st(dve.bn_aggr(mv[:, j, :], stats[:, j, :]))
                    st.wait()
                if prev:
                    norm_steps(Steps(dve, ln_step, LN_STEPS * (b - 1)), slice(0, TILES))
                    dve.wait_ge(ln_step, LN_STEPS * b)
                    dve.wait_ge(l_pe, b)
                    step(dve.tensor_tensor(logit[:, :, :], psS_l, ln[:, 1, 0:TILES][:, :, None].broadcast_to([P, TILES, E]), ALU.mult))
                if cur:
                    dve.wait_ge(ksT_pe, b + 1)
                    dve.wait_ge(n_pe, b)
                    dve.tensor_tensor(ksd[:, :, :], con("mask").rearrange("p (c h) -> p c h", h=H),
                                      psG_k[:, :, 0:1].broadcast_to([P, CH, H]), ALU.mult).then_inc(ks_done, 1)
                if prev:
                    choose()

                def gram_lo(h):
                    dve.wait_ge(g_h, 2 * b + h + 1)
                    cols = slice(h * 512, (h + 1) * 512)
                    lo(g_lo[:, cols], psG[:, h, :], g_hi[:, cols]).then_inc(g_l, 1)

                def mixed_lo(h):
                    cs = slice(h * CH // 2, (h + 1) * CH // 2)
                    dve.wait_ge(m_h, 2 * b + h + 1)
                    for a in range(2):
                        r = slice(DH * a, DH * (a + 1))
                        lo(m_lo[r, cs, :], psA_m[r, h, :, a, :], m_hi[r, cs, :]).then_inc((m_l0, m_l)[a], 1)

                if cur:
                    dve.wait_ge(n_pe, b + 1)
                    ns = Steps(dve, n_step, N_STEPS * b)
                    ns(dve.tensor_scalar(rn[:, 0, :], psS[0:H, :], NORM_EPS, None, ALU.add))
                if prev:
                    place()
                if cur:
                    ns.wait()
                    for h in range(2):
                        half = slice(h * S // 2, (h + 1) * S // 2)
                        ns(dve.reciprocal(rn[:, 1, half], rn[:, 0, half]))
                        gram_lo(h)
                    mixed_lo(0)
                    mixed_lo(1)
            batches(dve, attention)

            first_ = con("first", 1)
            dve.wait_ge(route, ROUTE_STEPS * B)
            tb = Steps(dve, tab_step, 0)
            tb(dve.tensor_tensor(cnt[:, 0, :], base[0:1, :], first_, ALU.subtract))
            tb.wait()
            tb(dve.tensor_tensor(full[:, :, :], cnt[:, 0, :][:, :, None].broadcast_to([1, E, 16]),
                                 con("step", 1).rearrange("p (e s) -> p e s", e=E), ALU.is_gt))
            tb.wait()
            tb(dve.tensor_reduce(cnt[:, 1, :], full[:, :, :], AX_X, ALU.add))
            tb.wait()
            tb(dve.tensor_tensor(upto_n[:, :, :], con("upto", 1).rearrange("p (a e) -> p a e", a=E),
                                 cnt[:, 1:2, :].broadcast_to([1, E, E]), ALU.mult))
            tb.wait()
            tb(dve.tensor_reduce(cnt[:, 2, :], upto_n[:, :, :], AX_X, ALU.add))
            tb.wait()
            tb(dve.tensor_tensor(past[:, 0, :, :], cnt[:, 2:3, :].broadcast_to([1, NBLK, E]),
                                 con("block", 1)[:, :, None].broadcast_to([1, NBLK, E]), ALU.is_le))
            tb.wait()
            tb(dve.tensor_reduce(tab[:, 0, :], past[:, 0, :, :], AX_X, ALU.add))
            tb(dve.tensor_tensor(past[:, 1, :, :], past[:, 0, :, :], cnt[:, 1:2, :].broadcast_to([1, NBLK, E]), ALU.mult))
            tb.wait()
            tb(dve.tensor_reduce(tab[:, 1, :], past[:, 1, :, :], AX_X, ALU.add))
            tb.wait()
            tb(dve.tensor_tensor(tab[:, 2, :], con("block", 1), tab[:, 1, :], ALU.subtract))
            tb.wait()
            tb(dve.tensor_scalar(tab[:, 3, :], tab[:, 2, :], float(BLK), None, ALU.mult))
            tb.wait()
            tb(dve.scalar_tensor_tensor(tab[:, 4, :], tab[:, 0, :], float(REGION), tab[:, 3, :], ALU.mult, ALU.add))
            tb.wait()
            dve.tensor_scalar(tabi[:, 0, :], tab[:, 0, :], float(E - 1), None, ALU.min).then_inc(table, 1)
            dve.tensor_scalar(tabi[:, 1, :], tab[:, 4, :], float(NOWHERE), None, ALU.min).then_inc(table, 1)

            def result(n, u, i):
                v = u % 2
                dve.wait_ge(e_down, n + 1)
                if later(n, SLOTS):
                    dve.wait_ge(e_out[u], 32 * i)
                dve.tensor_tensor(yrow[u][:, :, :], psY[v][:, :, :], b2_bc[u], ALU.add).then_inc(e_y0, 1)
                dve.wait_ge(e_y0, n + 1)
                dve.tensor_scalar(yrow[u][:, 0, :], yrow[u][:, 0, :], xrow[u][:, 0, D + 1:D + 2], None, ALU.mult).then_inc(e_y1, 1)
                dve.tensor_scalar(yrow[u][:, 1, :], yrow[u][:, 1, :], xrow[u][:, 1, D + 1:D + 2], None, ALU.mult).then_inc(e_y, 1)

            def experts(n, u, i):
                v = u % 2
                at, ws = slice(v * BLK, (v + 1) * BLK), slice(v * F, (v + 1) * F)
                dve.wait_ge(e_w[u], 16 * i + 16)
                if later(n, 2):
                    dve.wait_ge(e_up, FC * (n - 1))
                dve.tensor_copy(wq_hi[:, ws], w_raw[u][:, 0:F]).then_inc(e_wh, 1)
                dve.wait_ge(e_wh, n + 1)
                lo(wq_lo[:, ws], w_raw[u][:, 0:F], wq_hi[:, ws]).then_inc(e_wl, 1)
                dve.wait_ge(e_Th, n + 1)
                lo(xT_lo[:, at], psX[v], xT_hi[:, at]).then_inc(e_Tl, 1)
                if later(n, 2):
                    result(*earlier(n, u, i, 2))
            blocks(dve, experts)
            result(*last_blocks[0])
            result(*last_blocks[1])


            for g, at in groups:
                if g == B - LAST:
                    norm_steps(Steps(dve, f_ln, 0), slice(0, (B - LAST) * TILES))
                wait_alone(dve, f_z, g + 1)
                st = Steps(dve, f_stats, ST_STEPS * g)
                for t in range(g * TILES, (g + 1) * TILES):
                    st(dve.bn_stats(stats[:, t, :], psZ_t[t]))
                wait_alone(dve, st.which, st.n)
                for t in range(g * TILES, (g + 1) * TILES):
                    st(dve.bn_aggr(mv[:, t, :], stats[:, t, :]))
                st.wait()
            norm_steps(Steps(dve, f_ln, LN_STEPS), slice((B - LAST) * TILES, B * TILES))
            dve.wait_ge(f_ln, 2 * LN_STEPS)
            for t in range((B - LAST) * TILES, B * TILES):
                dve.tensor_scalar(yb[:, t, :], psZ_t[t], ln[:, 1, t:t + 1], ln[:, 3, t:t + 1],
                                  ALU.mult, ALU.add).then_inc(f_norm_dve, 1)


def kernel(L0_attn_x, L0_attn_W_qkv, L0_attn_W_f, L0_attn_b_f, L0_attn_W_out, L0_attn_b_out,
           L0_ffn_gate_w, L0_ffn_w1, L0_ffn_b1, L0_ffn_w2, L0_ffn_b2):
    import concourse.bacc as bacc
    from concourse.bass_utils import run_bass_kernel_spmd

    def f(a):
        return np.ascontiguousarray(a)
    x = np.asarray(L0_attn_x).reshape(N, D)
    w1 = np.transpose(np.asarray(L0_ffn_w1), (1, 2, 0))
    b1 = np.transpose(np.asarray(L0_ffn_b1).reshape(E, FC, P), (0, 2, 1))
    w2 = np.transpose(np.asarray(L0_ffn_w2).reshape(D, E, FC, P), (1, 3, 2, 0)).reshape(E, P, FC * D)
    b2 = np.broadcast_to(np.asarray(L0_ffn_b2)[:, None, :], (E, P, D))
    arrays = {
        "x": f(x), "xT": f(x.T), "wqkvT": f(np.asarray(L0_attn_W_qkv).T), "wf": f(L0_attn_W_f), "bf": f(L0_attn_b_f),
        "wout": f(L0_attn_W_out), "bout": f(L0_attn_b_out), "gwT": f(np.asarray(L0_ffn_gate_w).T),
        "w12": f(np.concatenate([w1, b1, w2, b2], axis=2)),
        "consts": shape_constants(),
    }
    nc = bacc.Bacc("TRN2", target_bir_lowering=False, num_devices=1)
    args = {n: nc.dram_tensor(n, a.shape, mybir.dt.from_np(a.dtype), kind="ExternalInput").ap() for n, a in arrays.items()}
    out = nc.dram_tensor("out", (B, S, D), F32, kind="ExternalOutput").ap()
    program(nc, out=out, **args)
    r = run_bass_kernel_spmd(nc, [arrays], core_ids=[0])
    return r.results[0]["out"]
```
